# Optimizing a Trainium2 kernel written in Bass

```python
import numpy as np
import jax
import jax.numpy as jnp

def _softmax(x, axis=-1):
    return jax.nn.softmax(x, axis=axis)
def _gelu(x):
    return jax.nn.gelu(x, approximate=True)
def _silu(x):
    return jax.nn.silu(x)
def _sigmoid(x):
    return jax.nn.sigmoid(x)
def _layernorm(x, axis=-1, eps=1e-5):
    m = jnp.mean(x, axis=axis, keepdims=True)
    v = jnp.var(x, axis=axis, keepdims=True)
    return (x - m) / jnp.sqrt(v + eps)
def _scatter_add(tgt, idx, src, axis=0):
    return tgt.at[idx].add(src)
def _segment_sum(src, seg, n):
    return jax.ops.segment_sum(src, seg, n)

kernel_name = 'mk_conv_preact_d1_conv_nchw384_a99822'

def setup_inputs(seed: int = 0):
    np.random.seed(seed)
    _w = jnp.asarray
    def _rec_inputs():
        import jax
        import jax.numpy as jnp
        _gk = jax.random.key(seed)
        x = 7.572e-06 + 1 * jax.random.normal(jax.random.fold_in(_gk, 1), (128, 384, 14, 14), jnp.float32)
        return x
    x = _rec_inputs()
    def _L0_conv_setup():
        import jax, jax.numpy as jnp
        import numpy as np
        RES = 14
        N = RES * RES
        NH = 8
        KD = 32
        D = 128
        DH = 1024
        DIM = 384
        B = 128
        SCALE = KD ** (-0.5)

        def _bias_idxs():
            pts = [(i, j) for i in range(RES) for j in range(RES)]
            offs, idxs = ({}, [])
            for p1 in pts:
                for p2 in pts:
                    o = (abs(p1[0] - p2[0]), abs(p1[1] - p2[1]))
                    offs.setdefault(o, len(offs))
                    idxs.append(offs[o])
            return (np.array(idxs, np.int32).reshape(N, N), len(offs))
        BIAS_IDXS, NUM_OFF = _bias_idxs()

        def _c(v):
            return v[None, :, None, None]

        def conv1x1_bn(x, w, b, s, t):
            y = jnp.einsum('bchw,oc->bohw', x, w) + _c(b)
            return y * _c(s) + _c(t)
        key = jax.random.key(seed)
        ks = jax.random.split(key, 32)
        g = lambda i, shape, s=0.05: jax.random.normal(ks[i], shape, jnp.float32) * s
        pos = lambda i, shape: jax.random.uniform(ks[i], shape, jnp.float32, minval=0.5, maxval=1.5)
        return dict(x=jax.random.normal(ks[0], (B, DIM, RES, RES), jnp.float32), qw=g(1, (NH * KD, DIM)), qb=g(2, (NH * KD,)), q_s=pos(3, (NH * KD,)), q_t=g(4, (NH * KD,)), kw=g(5, (NH * KD, DIM)), kb=g(6, (NH * KD,)), k_s=pos(7, (NH * KD,)), k_t=g(8, (NH * KD,)), vw=g(9, (DH, DIM)), vb=g(10, (DH,)), v_s=pos(11, (DH,)), v_t=g(12, (DH,)), lvw=g(13, (DH, 3, 3)), lvb=g(14, (DH,)), lv_s=pos(15, (DH,)), lv_t=g(16, (DH,)), th1w=g(17, (NH, NH), 0.3), th1b=g(18, (NH,)), th2w=g(19, (NH, NH), 0.3), th2b=g(20, (NH,)), ab=g(21, (NH, NUM_OFF)), pw=g(22, (DIM, DH)), pb=g(23, (DIM,)), p_s=pos(24, (DIM,)), p_t=g(25, (DIM,)))
    _L0_conv_all = _L0_conv_setup()
    _L0_conv_in = {k: v for k, v in _L0_conv_all.items() if k in ('qw', 'qb', 'q_s', 'q_t', 'kw', 'kb', 'k_s', 'k_t', 'vw', 'vb', 'v_s', 'v_t', 'lvw', 'lvb', 'lv_s', 'lv_t', 'th1w', 'th1b', 'th2w', 'th2b', 'ab', 'pw', 'pb', 'p_s', 'p_t', )}
    del _L0_conv_all

    return {
        "x": x,
        "L0_conv_qw": _L0_conv_in["qw"],
        "L0_conv_qb": _L0_conv_in["qb"],
        "L0_conv_q_s": _L0_conv_in["q_s"],
        "L0_conv_q_t": _L0_conv_in["q_t"],
        "L0_conv_kw": _L0_conv_in["kw"],
        "L0_conv_kb": _L0_conv_in["kb"],
        "L0_conv_k_s": _L0_conv_in["k_s"],
        "L0_conv_k_t": _L0_conv_in["k_t"],
        "L0_conv_vw": _L0_conv_in["vw"],
        "L0_conv_vb": _L0_conv_in["vb"],
        "L0_conv_v_s": _L0_conv_in["v_s"],
        "L0_conv_v_t": _L0_conv_in["v_t"],
        "L0_conv_lvw": _L0_conv_in["lvw"],
        "L0_conv_lvb": _L0_conv_in["lvb"],
        "L0_conv_lv_s": _L0_conv_in["lv_s"],
        "L0_conv_lv_t": _L0_conv_in["lv_t"],
        "L0_conv_th1w": _L0_conv_in["th1w"],
        "L0_conv_th1b": _L0_conv_in["th1b"],
        "L0_conv_th2w": _L0_conv_in["th2w"],
        "L0_conv_th2b": _L0_conv_in["th2b"],
        "L0_conv_ab": _L0_conv_in["ab"],
        "L0_conv_pw": _L0_conv_in["pw"],
        "L0_conv_pb": _L0_conv_in["pb"],
        "L0_conv_p_s": _L0_conv_in["p_s"],
        "L0_conv_p_t": _L0_conv_in["p_t"],
    }

def reference(x, L0_conv_qw, L0_conv_qb, L0_conv_q_s, L0_conv_q_t, L0_conv_kw, L0_conv_kb, L0_conv_k_s, L0_conv_k_t, L0_conv_vw, L0_conv_vb, L0_conv_v_s, L0_conv_v_t, L0_conv_lvw, L0_conv_lvb, L0_conv_lv_s, L0_conv_lv_t, L0_conv_th1w, L0_conv_th1b, L0_conv_th2w, L0_conv_th2b, L0_conv_ab, L0_conv_pw, L0_conv_pb, L0_conv_p_s, L0_conv_p_t):
    import jax
    import jax.numpy as jnp
    def _L0_conv_ref(x, qw, qb, q_s, q_t, kw, kb, k_s, k_t, vw, vb, v_s, v_t, lvw, lvb, lv_s, lv_t, th1w, th1b, th2w, th2b, ab, pw, pb, p_s, p_t):
        import jax, jax.numpy as jnp
        import numpy as np
        RES = 14
        N = RES * RES
        NH = 8
        KD = 32
        D = 128
        DH = 1024
        DIM = 384
        B = 128
        SCALE = KD ** (-0.5)

        def _bias_idxs():
            pts = [(i, j) for i in range(RES) for j in range(RES)]
            offs, idxs = ({}, [])
            for p1 in pts:
                for p2 in pts:
                    o = (abs(p1[0] - p2[0]), abs(p1[1] - p2[1]))
                    offs.setdefault(o, len(offs))
                    idxs.append(offs[o])
            return (np.array(idxs, np.int32).reshape(N, N), len(offs))
        BIAS_IDXS, NUM_OFF = _bias_idxs()

        def _c(v):
            return v[None, :, None, None]

        def conv1x1_bn(x, w, b, s, t):
            y = jnp.einsum('bchw,oc->bohw', x, w) + _c(b)
            return y * _c(s) + _c(t)
        Bb = x.shape[0]
        q = conv1x1_bn(x, qw, qb, q_s, q_t).reshape(Bb, NH, KD, N).transpose(0, 1, 3, 2)
        k = conv1x1_bn(x, kw, kb, k_s, k_t).reshape(Bb, NH, KD, N).transpose(0, 1, 3, 2)
        v4 = conv1x1_bn(x, vw, vb, v_s, v_t)
        vl = jax.lax.conv_general_dilated(v4, lvw.reshape(DH, 1, 3, 3), window_strides=(1, 1), padding='SAME', dimension_numbers=('NCHW', 'OIHW', 'NCHW'), feature_group_count=DH)
        vl = (vl + _c(lvb)) * _c(lv_s) + _c(lv_t)
        v = v4.reshape(Bb, NH, D, N).transpose(0, 1, 3, 2)
        attn = jnp.einsum('bhid,bhjd->bhij', q, k) * SCALE
        attn = attn + ab[:, BIAS_IDXS][None]
        attn = jnp.einsum('bhij,gh->bgij', attn, th1w) + _c(th1b)
        attn = jax.nn.softmax(attn, axis=-1)
        attn = jnp.einsum('bhij,gh->bgij', attn, th2w) + _c(th2b)
        o = jnp.einsum('bhij,bhjd->bhid', attn, v)
        o = o.transpose(0, 1, 3, 2).reshape(Bb, DH, RES, RES) + vl
        o = jax.nn.relu(o)
        return conv1x1_bn(o, pw, pb, p_s, p_t)

    def _gn(v, G=32, eps=1e-5):
        B_, C_, H_, W_ = v.shape
        g = v.reshape(B_, G, C_ // G, H_, W_)
        m = jnp.mean(g, axis=(2, 3, 4), keepdims=True)
        s = jnp.var(g, axis=(2, 3, 4), keepdims=True)
        return ((g - m) / jnp.sqrt(s + eps)).reshape(v.shape)

    def _ln_c(v, eps=1e-6):
        m = jnp.mean(v, axis=1, keepdims=True)
        s = jnp.var(v, axis=1, keepdims=True)
        return (v - m) / jnp.sqrt(s + eps)

    def _ln_t(v, eps=1e-5):
        m = jnp.mean(v, axis=-1, keepdims=True)
        s = jnp.var(v, axis=-1, keepdims=True)
        return (v - m) / jnp.sqrt(s + eps)

    def _to_tokens(v):
        B_, C_, H_, W_ = v.shape
        return v.reshape(B_, C_, H_ * W_).transpose(0, 2, 1)
    def _from_tokens(t, like):
        B_, C_, H_, W_ = like.shape
        return t.transpose(0, 2, 1).reshape(B_, C_, H_, W_)

    x = x + _L0_conv_ref(_gn(x), L0_conv_qw, L0_conv_qb, L0_conv_q_s, L0_conv_q_t, L0_conv_kw, L0_conv_kb, L0_conv_k_s, L0_conv_k_t, L0_conv_vw, L0_conv_vb, L0_conv_v_s, L0_conv_v_t, L0_conv_lvw, L0_conv_lvb, L0_conv_lv_s, L0_conv_lv_t, L0_conv_th1w, L0_conv_th1b, L0_conv_th2w, L0_conv_th2b, L0_conv_ab, L0_conv_pw, L0_conv_pb, L0_conv_p_s, L0_conv_p_t)
    return x


_drawn_inputs = setup_inputs


def setup_inputs(seed=0):
    import zlib

    import numpy as np

    out = dict(_drawn_inputs(seed))
    spreads = {}
    factors = {'L0_conv_qb': 8.0,
     'L0_conv_q_s': 3.712,
     'L0_conv_q_t': 8.0,
     'L0_conv_kb': 8.0,
     'L0_conv_k_s': 3.481,
     'L0_conv_k_t': 8.0,
     'L0_conv_th1b': 8.0,
     'L0_conv_ab': 8.0}
    for name, (base, spread) in spreads.items():
        noise = np.random.default_rng([zlib.crc32(name.encode()), seed]).standard_normal(out[name].shape)
        drawn = base * np.exp(spread * noise) if base else spread * noise
        out[name] = jnp.asarray(drawn.astype(out[name].dtype))
    for name, factor in factors.items():
        out[name] = (out[name] * factor).astype(out[name].dtype)
    return out
```

```python
import numpy as np
import concourse.bass as bass
from concourse import mybir
from contextlib import ExitStack

BATCH, DIM, RES = 128, 384, 14
PIX = RES * RES
NH, KD, D = 8, 32, 128
DH = NH * D
GROUPS, GC = 32, DIM // 32
P = 128
PAIRS = BATCH // 2
CT = DIM // P
QT = NH * KD // P
VT = DH // P
COLS = 2 * PIX
HP = NH * RES
PITCH = RES + 1
HALF = RES // 2 * PITCH
HR = P // KD
VPAD = 32 * PITCH
ACC_ROWS = 2 * RES + 1
IMG = (RES + 1) * RES
ACC = ACC_ROWS * RES
WINDOW = (2 * RES - 1) * RES
BANK = 512
TAPS = [k for k in range(9) if k != 4]
SCALE = KD ** -0.5
EPS = 1e-5
NPAR = 3 * 12 + 3 * CT + 3 * VT + 9 * VT


def build(nc, A, out):
    f32, f32r = mybir.dt.float32, mybir.dt.float32r
    ALU, ACT = mybir.AluOpType, mybir.ActivationFunctionType
    MUL, ADD, SUB = ALU.mult, ALU.add, ALU.subtract

    with ExitStack() as ctx:
        def sb(name, shape, dt=f32):
            return ctx.enter_context(nc.sbuf_tensor(name, shape, dt))

        def sem(name):
            return ctx.enter_context(nc.semaphore(name))

        w_hi = sb("w_hi", [P, CT, 12 * P], f32r)
        w_lo = sb("w_lo", [P, CT, 12 * P], f32r)
        wp_hi = sb("wp_hi", [P, VT, DIM], f32r)
        wp_lo = sb("wp_lo", [P, VT, DIM], f32r)
        par = sb("par", [P, NPAR])
        th1 = sb("th1", [P, QT, NH])
        bias = sb("bias", [HP, WINDOW])
        kron2 = sb("kron2", [HP, NH, RES])
        ident = sb("ident", [P, P])
        g_sum = sb("g_sum", [P, CT, GROUPS])
        g_bc = sb("g_bc", [GROUPS, CT, P])
        small = sb("small", [HP, 2 * NH + RES + 1])
        abx = sb("abx", [HP, WINDOW])
        kron1 = sb("kron1", [HP, NH, RES])
        mhalf = sb("mhalf", [GROUPS, 2])
        xs = sb("xs", [P, CT, 2, PIX])
        bst = sb("bst", [P, 2 * CT, 6])
        mv = sb("mv", [P, 2 * CT, 2])
        mean_sq = sb("mean_sq", [P, 2 * CT])
        gs = sb("gs", [GROUPS, 2, 2])
        g_msq = sb("g_msq", [GROUPS, 2])
        g_var = sb("g_var", [GROUPS, 2])
        g_val = sb("g_val", [GROUPS, 2, 2])
        ab = sb("ab", [P, CT, 2, 2])
        x_hi = sb("x_hi", [P, CT, COLS], f32r)
        x_lo = sb("x_lo", [P, CT, COLS], f32r)
        q = sb("q", [P, QT, COLS])
        k = sb("k", [P, QT, COLS])
        qa = sb("qa", [P, 4 * RES * HP])
        probs = sb("probs", [P, 2, RES, 2 * HALF])
        nmax = sb("nmax", [HP, 2, RES])
        rowsum = sb("rowsum", [HP, 2, RES])
        rinv = sb("rinv", [HP, 2, RES])
        mixw = sb("mixw", [P, 2, RES, HP])
        vpad = sb("vpad", [P, VT, VPAD])
        vt = sb("vt", [P, 2, DH])
        acc = sb("acc", [P, VT, ACC])
        o_hi = sb("o_hi", [P, VT, COLS], f32r)
        o_lo = sb("o_lo", [P, VT, COLS], f32r)
        res = sb("res", [P, CT, COLS])
        psA = ctx.enter_context(nc.psum_tensor("psA", [P, 2, BANK], f32))
        psL = ctx.enter_context(nc.psum_tensor("psL", [P, 2, BANK], f32))
        psM = ctx.enter_context(nc.psum_tensor("psM", [P, 2, BANK], f32))
        psP = ctx.enter_context(nc.psum_tensor("psP", [P, 2, BANK], f32))

        qmix = qa[:, :].rearrange("p (k b m) -> p k b m", k=QT, b=2 * RES)
        attn = qa[0:HALF, :].rearrange("p (i j g n) -> p i j g n", i=2, j=2, g=NH)
        stage_w = qa[:, 0:CT * 12 * P].rearrange("p (k m) -> p k m", k=CT)
        stage_p = acc[:, :, :].rearrange("p c n -> p (c n)")[:, 0:VT * DIM].rearrange("p (k m) -> p k m", k=VT)

        at = [0]

        def part(n, groups):
            v = par[:, at[0]:at[0] + n * groups]
            at[0] += n * groups
            return v.rearrange("p (a c) -> p a c", a=groups) if groups > 1 else v
        qkv_b, qkv_s, qkv_t = part(12, 1), part(12, 1), part(12, 1)
        p_b, p_s, p_t = part(CT, 1), part(CT, 1), part(CT, 1)
        l_b, l_s, l_t = part(VT, 1), part(VT, 1), part(VT, 1)
        taps = part(9, VT)
        th1r, th2r = small[:, 0:NH], small[:, NH:2 * NH]
        delta, th1b = small[:, 2 * NH:2 * NH + RES], small[:, 2 * NH + RES:2 * NH + RES + 1]

        x_pairs = A["x"].rearrange("(t i) (k p) n -> t k p i n", i=2, p=P)
        o_pairs = out.rearrange("(t i) (k p) n -> t k p i n", i=2, p=P)

        s_w, s_wp, s_par = sem("s_w"), sem("s_wp"), sem("s_par")
        s_x, s_res = sem("s_x"), sem("s_res")
        s_store = sem("s_store")
        s_kron1, s_kron2, s_c = sem("s_kron1"), sem("s_kron2"), sem("s_c")
        s_whi, s_prep, s_zero, s_biasmm = sem("s_whi"), sem("s_prep"), sem("s_zero"), sem("s_biasmm")
        s_ready = sem("s_ready")
        s_v_mm, s_qk_mm, s_proj_mm = sem("s_v_mm"), sem("s_qk_mm"), sem("s_proj_mm")
        s_logit_mm, s_vt_mm, s_mix_mm, s_av_mm = sem("s_logit_mm"), sem("s_vt_mm"), sem("s_mix_mm"), sem("s_av_mm")
        s_gsum_mm, s_gbc_mm = sem("s_gsum_mm"), sem("s_gbc_mm")
        s_v_sb, s_conv0, s_qk_sb, s_exp = sem("s_v_sb"), sem("s_conv0"), sem("s_qk_sb"), sem("s_exp")
        s_xhi, s_vt_sb, s_mix_sb, s_relu = sem("s_xhi"), sem("s_vt_sb"), sem("s_mix_sb"), sem("s_relu")
        s_conv, s_score, s_rinv = sem("s_conv"), sem("s_score"), sem("s_rinv")
        s_out, s_add, s_olo = sem("s_out"), sem("s_add"), sem("s_olo")
        s_bst, s_mv, s_msq, s_stat = sem("s_bst"), sem("s_mv"), sem("s_msq"), sem("s_stat")
        s_gs, s_gmsq, s_gvar, s_gval, s_ab, s_xn = (sem(n) for n in ("s_gs", "s_gmsq", "s_gvar", "s_gval", "s_ab", "s_xn"))
        s_qmix, s_resb, s_rstd, s_xlo, s_mixw = sem("s_qmix"), sem("s_resb"), sem("s_rstd"), sem("s_xlo"), sem("s_mixw")

        block = ctx.enter_context(nc.Block())
        N_PAR_DMA = 9

        def keys(img, b):
            return probs[0:HP, img, b, :].rearrange("p (r w) -> p r w", w=PITCH)[:, :, 0:RES]

        def group(b):
            return b // 4

        def wait_alone(eng, semaphore, value):
            eng.wait_ge(semaphore, value)
            eng.nop(nofuse=True)

        def rounds(eng, step):
            step(0, True, False)
            with eng.Fori(1, PAIRS - 1) as t:
                step(t, False, False)
            step(PAIRS - 1, False, True)

        @block.sync
        def _(sp):
            sp.dma_start(stage_w, A["wqkv"].rearrange("(k p) m -> p k m", p=P)).then_inc(s_w, 16)
            for kt in range(CT):
                sp.dma_start(xs[:, kt, :, :], x_pairs[0, kt]).then_inc(s_x, 16)
            sp.dma_start(stage_p, A["wp"].rearrange("(k p) m -> p k m", p=P)).then_inc(s_wp, 16)
            sp.wait_ge(s_zero, 1)
            for dst, src in ((par[:, :], A["par"]), (th1[:, :, :], A["th1"]), (ident[:, :], A["ident"]),
                             (g_sum[:, :, :], A["g_sum"]), (g_bc[:, :, :], A["g_bc"]), (small[:, :], A["small"]),
                             (abx[:, :], A["abx"]),
                             (mixw[HP:HP + 1, 0, :, :], A["th2b"]), (mixw[HP:HP + 1, 1, :, :], A["th2b"])):
                sp.dma_start(dst, src).then_inc(s_par, 16)

            def residual(t):
                for kt in range(CT):
                    sp.dma_start(res[:, kt, :].rearrange("p (i n) -> p i n", i=2),
                                 x_pairs[t - 1, kt]).then_inc(s_res, 16)

            def store(t):
                for kt in range(CT):
                    sp.wait_ge(s_out, 3 * (t - 1) + kt + 2)
                    sp.dma_start(o_pairs[t - 1, kt],
                                 res[:, kt, :].rearrange("p (i n) -> p i n", i=2)).then_inc(s_store, 16)
                wait_alone(sp, s_store, 48 * t)

            def step(t, first, last):
                if not first:
                    residual(t)
                if not last:
                    sp.wait_ge(s_xhi, t + 1)
                    sp.wait_ge(s_xlo, t + 1)
                    for kt in range(CT):
                        sp.dma_start(xs[:, kt, :, :], x_pairs[t + 1, kt]).then_inc(s_x, 16)
                if not first:
                    store(t)
            rounds(sp, step)
            residual(PAIRS)
            store(PAIRS)

        @block.tensor
        def _(pe):
            def split3(dst, terms, hi, lo, m0, rhi, rlo):
                for c in range(terms):
                    for n, (w, r) in enumerate(((lo, rhi), (hi, rlo), (hi, rhi))):
                        last = nc.tensor.matmul(dst, w[:, c, m0:m0 + P], r[:, c, :], start=(c == 0 and n == 0),
                                                stop=(c == terms - 1 and n == 2))
                return last

            def group_sums(p):
                pe.wait_ge(s_stat, p + 1)
                for kt in range(CT):
                    last = nc.tensor.matmul(psP[0:GROUPS, 1, 0:4], g_sum[:, kt, :],
                                            mv[:, 2 * kt:2 * kt + 2, :].rearrange("p i s -> p (i s)"),
                                            start=(kt == 0), stop=(kt == CT - 1))
                last.then_inc(s_gsum_mm, 1)

            def group_broadcast(p):
                pe.wait_ge(s_gval, p + 1)
                for kt in range(CT):
                    last = nc.tensor.matmul(psP[:, 1, 8 + 4 * kt:12 + 4 * kt], g_bc[:, kt, :],
                                            g_val[:, :, :].rearrange("p i s -> p (i s)"), start=True, stop=True)
                last.then_inc(s_gbc_mm, 1)

            def project(t):
                for m in range(CT):
                    if m == 0:
                        pe.wait_ge(s_relu, 8 * t)
                        pe.wait_ge(s_olo, 8 * t)
                        pe.wait_ge(s_out, 3 * (t - 1) + 1)
                    elif m == 1:
                        pe.wait_ge(s_ab, min(t + 1, PAIRS) if isinstance(t, int) else t + 1)
                    else:
                        pe.wait_ge(s_out, 3 * (t - 1) + 2)
                    split3(psP[:, m % 2, 0:COLS], VT, wp_hi, wp_lo, m * P, o_hi, o_lo).then_inc(s_proj_mm, 1)

            pe.wait_ge(s_kron1, 1)
            nc.tensor.matmul(psP[0:HP, 0, 0:WINDOW], kron1[:, :, :].rearrange("p g i -> p (g i)"), abx[:, :],
                             start=True, stop=True).then_inc(s_biasmm, 1)
            group_sums(0)
            group_broadcast(0)
            pe.wait_ge(s_prep, 2)

            def step(t, first, last):
                pe.wait_ge(s_xhi, t + 1)
                pe.wait_ge(s_xlo, t + 1)
                for m in range(VT):
                    if m >= 2:
                        pe.wait_ge(s_v_sb, VT * t + m - 1)
                    elif not first:
                        pe.wait_ge(s_add, 8 * t - 1 + m)
                    split3(psA[:, m % 2, 0:COLS], CT, w_hi, w_lo, (4 + m) * P, x_hi, x_lo).then_inc(s_v_mm, 1)
                for m in range(4):
                    if m >= 2:
                        pe.wait_ge(s_qk_sb, 4 * t + m - 1)
                    else:
                        pe.wait_ge(s_v_sb, VT * t + 7 + m)
                    split3(psA[:, m % 2, 0:COLS], CT, w_hi, w_lo, m * P, x_hi, x_lo).then_inc(s_qk_mm, 1)
                if not first:
                    project(t)
                if not last:
                    if not first:
                        pe.wait_ge(s_out, 3 * (t - 1) + 3)
                    group_sums(t + 1)
                pe.wait_ge(s_qk_sb, 4 * (t + 1))
                pe.wait_ge(s_qmix, 16 * (t + 1))
                for n in range(RES):
                    img, b0 = n // 7, 2 * (n % 7)
                    if n >= 2 or not first:
                        pe.wait_ge(s_score, 28 * t + 2 * n - 2)
                    for b in (b0, b0 + 1):
                        for kt in range(QT):
                            mm = nc.tensor.matmul(psL[0:HP, n % 2, (b - b0) * PIX:(b - b0 + 1) * PIX],
                                                  qmix[:, kt, img * RES + b, :], k[:, kt, img * PIX:(img + 1) * PIX],
                                                  start=(kt == 0), stop=(kt == QT - 1))
                    mm.then_inc(s_logit_mm, 1)
                    if n == 6 and not last:
                        group_broadcast(t + 1)
                for img in range(2):
                    use = 11 * img

                    def bank_free(use):
                        ago = use - 2
                        tt = t
                        if ago < 0:
                            if first:
                                return
                            ago, tt = ago + 22, t - 1
                        i, n = divmod(ago, 11)
                        if n < 4:
                            pe.wait_ge(s_vt_sb, 8 * tt + 4 * i + n + 1)
                        else:
                            pe.wait_ge(s_mix_sb, 14 * tt + 7 * i + n - 3)

                    for n in range(4):
                        jc, cg = divmod(n, 2)
                        bank_free(use)
                        for c in range(4):
                            at_ = PITCH + 1 + img * PITCH * PITCH + jc * (RES // 2) * PITCH
                            mm = nc.tensor.transpose(psM[0:HALF, use % 2, c * P:(c + 1) * P],
                                                     vpad[:, 4 * cg + c, at_:at_ + HALF], ident[:, :])
                        mm.then_inc(s_vt_mm, 1)
                        use += 1
                    for n in range(7):
                        bank_free(use)
                        pe.wait_ge(s_exp, 28 * t + 14 * img + 2 * n + 2)
                        pe.wait_ge(s_mixw, 8 * t + 4 * img + group(2 * n + 1) + 1)
                        bank = psM[0:HALF, use % 2, 0:4 * HP].rearrange("p (j g b i) -> p j g b i", j=2, g=NH, b=2)
                        for jc in range(2):
                            for b in range(2):
                                mm = nc.tensor.matmul(bank[:, jc, :, b, :],
                                                      probs[0:HP + 1, img, 2 * n + b, jc * HALF:(jc + 1) * HALF],
                                                      mixw[0:HP + 1, img, 2 * n + b, :].rearrange("p (g i) -> p g i", g=NH),
                                                      start=True, stop=True)
                        mm.then_inc(s_mix_mm, 1)
                        use += 1
                    pe.wait_ge(s_vt_sb, 8 * t + 4 * img + 4)
                    pe.wait_ge(s_mix_sb, 14 * t + 7 * img + 7)
                    for n in range(4):
                        u = 4 * img + n
                        if u < 2:
                            pe.wait_ge(s_qk_sb, 4 * t + 3 + u)
                        else:
                            pe.wait_ge(s_add, 8 * t + u - 1)
                        for e in range(2):
                            g = 2 * n + e
                            for jc in range(2):
                                mm = nc.tensor.matmul(psA[:, u % 2, e * PIX:(e + 1) * PIX],
                                                      vt[0:HALF, jc, g * D:(g + 1) * D], attn[:, img, jc, g, :],
                                                      start=(jc == 0), stop=(jc == 1))
                        mm.then_inc(s_av_mm, 1)
            rounds(pe, step)
            project(PAIRS)

        @block.scalar
        def _(act):
            act.wait_ge(s_w, 16)
            nc.scalar.copy(w_hi[:, :, :], stage_w).then_inc(s_whi, 1)
            act.wait_ge(s_wp, 16)
            nc.scalar.copy(wp_hi[:, :, :], stage_p).then_inc(s_whi, 1)

            def x_high(p):
                act.wait_ge(s_xn, 6 * (p + 1))
                nc.scalar.copy(x_hi[:, :, :], xs[:, :, :, :].rearrange("p k i n -> p k (i n)")).then_inc(s_xhi, 1)
            x_high(0)

            def conv_centre(t, c):
                act.wait_ge(s_v_sb, VT * t + c + 1)
                src = vpad[:, c, PITCH + 1:PITCH + 1 + ACC_ROWS * PITCH].rearrange("p (r w) -> p r w", w=PITCH)
                nc.scalar.activation(acc[:, c, :].rearrange("p (r w) -> p r w", w=RES), src[:, :, 0:RES],
                                     ACT.Identity, bias=l_t[:, c:c + 1], scale=taps[:, c, 4:5]).then_inc(s_conv0, 1)

            def relu(t, img, n):
                act.wait_ge(s_add, 8 * t + 4 * img + n + 1)
                nc.scalar.activation(o_hi[:, 2 * n:2 * n + 2, img * PIX:(img + 1) * PIX],
                                     acc[:, 2 * n:2 * n + 2, img * IMG:img * IMG + PIX], ACT.Relu).then_inc(s_relu, 1)

            act.wait_ge(s_ready, 1)

            def step(t, first, last):
                if not first:
                    act.wait_ge(s_vt_mm, 8 * t)
                    act.wait_ge(s_conv, 64 * t)
                    act.wait_ge(s_olo, 8 * t)
                else:
                    act.wait_ge(s_prep, 2)
                for m in range(VT):
                    act.wait_ge(s_v_mm, VT * t + m + 1)
                    at_ = PITCH + 1
                    dst = vpad[:, m, at_:at_ + 2 * PITCH * PITCH].rearrange("p (i r w) -> p i r w", i=2, w=PITCH)
                    nc.scalar.activation(dst[:, :, 0:RES, 0:RES],
                                         psA[:, m % 2, 0:COLS].rearrange("p (i r w) -> p i r w", i=2, w=RES),
                                         ACT.Identity, bias=qkv_t[:, 4 + m:5 + m],
                                         scale=qkv_s[:, 4 + m:5 + m]).then_inc(s_v_sb, 1)
                    if m:
                        conv_centre(t, m - 1)
                conv_centre(t, VT - 1)
                for m in range(4):
                    act.wait_ge(s_qk_mm, 4 * t + m + 1)
                    if m == 0 and not first:
                        act.wait_ge(s_qmix, 16 * t)
                    if m == 2 and not first:
                        act.wait_ge(s_logit_mm, 14 * t)
                    dst = (q if m < 2 else k)[:, m % 2, :]
                    nc.scalar.activation(dst, psA[:, m % 2, 0:COLS], ACT.Identity, bias=qkv_t[:, m:m + 1],
                                         scale=qkv_s[:, m:m + 1]).then_inc(s_qk_sb, 1)
                if not first:
                    act.wait_ge(s_rinv, 2 * t)
                for n in range(2 * RES):
                    img, b = divmod(n, RES)
                    act.wait_ge(s_score, 28 * t + n + 1)
                    row = keys(img, b)
                    nc.scalar.activation(row, row, ACT.Exp,
                                         bias=nmax[:, img, b:b + 1], scale=-1.0,
                                         accum_out=rowsum[:, img, b:b + 1]).then_inc(s_exp, 1)
                if not last:
                    act.wait_ge(s_qk_mm, 4 * (t + 1))
                    x_high(t + 1)
                for img in range(2):
                    for n in range(4):
                        jc, cg = divmod(n, 2)
                        act.wait_ge(s_vt_mm, 8 * t + 4 * img + n + 1)
                        if n == 0 and (img or not first):
                            act.wait_ge(s_av_mm, 8 * t + 4 * img)
                        nc.scalar.copy(vt[0:HALF, jc, cg * BANK:(cg + 1) * BANK],
                                       psM[0:HALF, (11 * img + n) % 2, :]).then_inc(s_vt_sb, 1)
                    for n in range(7):
                        act.wait_ge(s_mix_mm, 14 * t + 7 * img + n + 1)
                        src = psM[0:HALF, (11 * img + 4 + n) % 2, 0:4 * HP].rearrange("p (j g m) -> p j g m", j=2, g=NH)
                        nc.scalar.copy(attn[:, img, :, :, 2 * n * RES:(2 * n + 2) * RES], src).then_inc(s_mix_sb, 1)
                    if img == 0 and not first:
                        act.wait_ge(s_proj_mm, 3 * t)
                    for n in range(4):
                        relu(t, img, n)
            rounds(act, step)

        @block.vector
        def _(dve):
            nc.vector.memset(mixw[:, :, :, :], 0.0).then_inc(s_zero, 1)
            nc.vector.memset(probs[:, :, :, :], 1.0)
            nc.vector.memset(vpad[:, :, :], 0.0)
            nc.vector.memset(mhalf[:, :], -0.5)
            dve.wait_ge(s_par, 16 * N_PAR_DMA)
            for dst, src, signal in ((kron2, th2r, s_kron2), (kron1, th1r, s_kron1)):
                nc.vector.tensor_tensor(dst[:, :, :], src.unsqueeze(2).broadcast_to([HP, NH, RES]),
                                        delta.unsqueeze(1).broadcast_to([HP, NH, RES]), MUL).then_inc(signal, 1)
            nc.vector.tensor_tensor(qkv_b, qkv_b, qkv_s, MUL)
            nc.vector.tensor_tensor(p_b, p_b, p_s, MUL)
            nc.vector.tensor_tensor(l_b, l_b, l_s, MUL)
            nc.vector.tensor_tensor(taps, taps, l_s.unsqueeze(2).broadcast_to([P, VT, 9]), MUL).then_inc(s_c, 1)
            dve.wait_ge(s_c, 1)
            nc.vector.tensor_tensor(qkv_t, qkv_t, qkv_b, ADD)
            nc.vector.tensor_tensor(p_t, p_t, p_b, ADD)
            nc.vector.tensor_tensor(l_t, l_t, l_b, ADD).then_inc(s_ready, 1)

            def stats(p):
                dve.wait_ge(s_x, 48 * (p + 1))
                for n in range(2 * CT):
                    nc.vector.bn_stats(bst[:, n, :], xs[:, n // 2, n % 2, :]).then_inc(s_bst, 1)
                wait_alone(dve, s_bst, 6 * (p + 1))
                for n in range(2 * CT):
                    nc.vector.bn_aggr(mv[:, n, :], bst[:, n, :]).then_inc(s_mv, 1)
                dve.wait_ge(s_mv, 6 * (p + 1))
                nc.vector.tensor_tensor(mean_sq[:, :], mv[:, :, 0], mv[:, :, 0], MUL).then_inc(s_msq, 1)
                dve.wait_ge(s_msq, p + 1)
                nc.vector.tensor_tensor(mv[:, :, 1], mv[:, :, 1], mean_sq[:, :], ADD).then_inc(s_stat, 1)

            def group_variance(p):
                dve.wait_ge(s_gsum_mm, p + 1)
                nc.vector.tensor_copy(gs[:, :, :].rearrange("p i s -> p (i s)"), psP[0:GROUPS, 1, 0:4]).then_inc(s_gs, 1)
                dve.wait_ge(s_gs, p + 1)
                nc.vector.tensor_tensor(g_msq[:, :], gs[:, :, 0], gs[:, :, 0], MUL).then_inc(s_gmsq, 1)
                dve.wait_ge(s_gmsq, p + 1)
                nc.vector.scalar_tensor_tensor(g_var[:, :], gs[:, :, 1], EPS, g_msq[:, :], ADD, SUB).then_inc(s_gvar, 1)

            def group_values(p):
                dve.wait_ge(s_rstd, p + 1)
                nc.vector.scalar_tensor_tensor(g_val[:, :, 1], gs[:, :, 0], -1.0, g_val[:, :, 0], MUL, MUL).then_inc(s_gval, 1)

            def channel_values(p):
                dve.wait_ge(s_gbc_mm, p + 1)
                nc.vector.tensor_copy(ab[:, :, :, :].rearrange("p k i s -> p (k i s)"), psP[:, 1, 8:20]).then_inc(s_ab, 1)

            def normalise(p, n):
                kt, i = divmod(n, 2)
                dve.wait_ge(s_ab, p + 1)
                nc.vector.tensor_scalar(xs[:, kt, i, :], xs[:, kt, i, :], ab[:, kt, i, 0:1], ab[:, kt, i, 1:2],
                                        MUL, ADD).then_inc(s_xn, 1)

            stats(0)
            group_variance(0)
            group_values(0)
            channel_values(0)
            for n in range(6):
                normalise(0, n)
            dve.wait_ge(s_whi, 1)
            nc.vector.tensor_tensor(w_lo[:, :, :], stage_w, w_hi[:, :, :].bitcast(f32), SUB).then_inc(s_prep, 1)
            dve.wait_ge(s_whi, 2)
            nc.vector.tensor_tensor(wp_lo[:, :, :], stage_p, wp_hi[:, :, :].bitcast(f32), SUB).then_inc(s_prep, 1)
            dve.wait_ge(s_biasmm, 1)
            nc.vector.tensor_scalar(bias[:, :], psP[0:HP, 0, 0:WINDOW], th1b, None, ADD).then_inc(s_out, 1)

            def conv(t, first, c0, n):
                tap, e = divmod(n, 2)
                c = c0 + e
                if tap == 0:
                    dve.wait_ge(s_conv0, VT * t + c + 1)
                else:
                    dve.wait_ge(s_conv, 64 * t + 8 * c0 + 2 * (tap - 1) + e + 1)
                dy, dx = divmod(TAPS[tap], 3)
                at_ = dy * PITCH + dx
                src = vpad[:, c, at_:at_ + ACC_ROWS * PITCH].rearrange("p (r w) -> p r w", w=PITCH)[:, :, 0:RES]
                a = acc[:, c, :].rearrange("p (r w) -> p r w", w=RES)
                nc.vector.scalar_tensor_tensor(a, src, taps[:, c, TAPS[tap]:TAPS[tap] + 1], a, MUL, ADD).then_inc(s_conv, 1)

            def project_out(t, m):
                dve.wait_ge(s_resb, 3 * (t - 1) + m + 1)
                dve.wait_ge(s_proj_mm, 3 * (t - 1) + m + 1)
                nc.vector.scalar_tensor_tensor(res[:, m, :], psP[:, m % 2, 0:COLS], p_s[:, m:m + 1], res[:, m, :],
                                               MUL, ADD).then_inc(s_out, 1)

            def step(t, first, last):
                todo = iter([(c, n) for c in range(0, VT, 2) for n in range(16)])

                def convs(count):
                    for _ in range(count):
                        nxt = next(todo, None)
                        if nxt:
                            conv(t, first, *nxt)

                convs(32)
                if not last:
                    stats(t + 1)
                if not first:
                    project_out(t, 0)
                convs(8)
                if not first:
                    project_out(t, 1)
                convs(5)
                if not first:
                    project_out(t, 2)
                if first:
                    dve.wait_ge(s_out, 1)
                if not first:
                    dve.wait_ge(s_mix_mm, 14 * t)
                for n in range(RES):
                    wait_alone(dve, s_logit_mm, 14 * t + n + 1)
                    for r in (2 * n, 2 * n + 1):
                        img, b = divmod(r, RES)
                        at_ = (RES - 1 - b) * RES
                        nc.vector.tensor_tensor_reduce(
                            out=keys(img, b),
                            in0=psL[0:HP, n % 2, (r % 2) * PIX:(r % 2 + 1) * PIX].rearrange("p (r w) -> p r w", w=RES),
                            in1=bias[:, at_:at_ + PIX].rearrange("p (r w) -> p r w", w=RES), scale=-1.0, scalar=3.4028234e38, op0=ADD, op1=ALU.min,
                            accum_out=nmax[:, img, b:b + 1]).then_inc(s_score, 1)
                    if n == 0 and not last:
                        group_variance(t + 1)
                    elif n == 3 and not last:
                        group_values(t + 1)
                    elif n == 8 and not last:
                        channel_values(t + 1)
                    elif n == 9:
                        dve.wait_ge(s_exp, 28 * t + 14)
                        if not first:
                            dve.wait_ge(s_mixw, 8 * t)
                        nc.vector.reciprocal(rinv[:, 0, :], rowsum[:, 0, :]).then_inc(s_rinv, 1)
                    if n >= 10 and not last:
                        normalise(t + 1, n - 10)
                    convs(1)
                if not last:
                    normalise(t + 1, 4)
                    normalise(t + 1, 5)
                dve.wait_ge(s_exp, 28 * t + 28)
                nc.vector.reciprocal(rinv[:, 1, :], rowsum[:, 1, :]).then_inc(s_rinv, 1)
                convs(64)
                if not first:
                    dve.wait_ge(s_proj_mm, 3 * t)

                def low(img, n):
                    dve.wait_ge(s_relu, 8 * t + 4 * img + n + 1)
                    a = acc[:, 2 * n:2 * n + 2, img * IMG:img * IMG + PIX]
                    sl = (slice(None), slice(2 * n, 2 * n + 2), slice(img * PIX, (img + 1) * PIX))
                    nc.vector.scalar_tensor_tensor(o_lo[sl], a, 0.0, o_hi[sl].bitcast(f32), ALU.max, SUB).then_inc(s_olo, 1)

                for img in range(2):
                    for n in range(4):
                        dve.wait_ge(s_conv, 64 * t + 16 * (n + 1))
                        dve.wait_ge(s_av_mm, 8 * t + 4 * img + n + 1)
                        a = acc[:, 2 * n:2 * n + 2, img * IMG:img * IMG + PIX]
                        nc.vector.tensor_tensor(a, psA[:, n % 2, 0:COLS].rearrange("p (c n) -> p c n", c=2), a,
                                                ADD).then_inc(s_add, 1)
                        if n:
                            low(img, n - 1)
                    low(img, 3)
            rounds(dve, step)
            for m in range(CT):
                project_out(PAIRS, m)

        @block.gpsimd
        def _(pool):
            pool.wait_ge(s_ready, 1)

            def rstd(p):
                pool.wait_ge(s_gvar, p + 1)
                nc.gpsimd.tensor_tensor(g_val[:, :, 0], g_var[:, :], mhalf[:, :], ALU.pow).then_inc(s_rstd, 1)

            def x_low(p):
                pool.wait_ge(s_xhi, p + 1)
                nc.gpsimd.tensor_tensor(x_lo[:, :, :], xs[:, :, :, :].rearrange("p k i n -> p k (i n)"),
                                        x_hi[:, :, :].bitcast(f32), SUB).then_inc(s_xlo, 1)

            def residual_bias(t):
                wait_alone(pool, s_res, 48 * t)
                for m in range(CT):
                    nc.gpsimd.tensor_scalar(res[:, m, :], res[:, m, :], p_t[:, m:m + 1], 1.0, ADD, MUL).then_inc(s_resb, 1)

            def mixing_weights(t, first, img):
                if not first:
                    pool.wait_ge(s_mix_mm, 14 * (t - 1) + 7 * (img + 1))
                pool.wait_ge(s_rinv, 2 * t + img + 1)
                for b0 in range(0, RES, 4):
                    nb = min(4, RES - b0)
                    k2 = kron2[:, :, :].rearrange("p g i -> p (g i)").unsqueeze(1).broadcast_to([HP, nb, HP])
                    nc.gpsimd.tensor_tensor(mixw[0:HP, img, b0:b0 + nb, :], k2,
                                            rinv[:, img, b0:b0 + nb].unsqueeze(2).broadcast_to([HP, nb, HP]),
                                            MUL).then_inc(s_mixw, 1)

            rstd(0)
            x_low(0)
            pool.wait_ge(s_prep, 1)

            def step(t, first, last):
                if not first:
                    residual_bias(t)
                    pool.wait_ge(s_av_mm, 8 * t)
                for kt in range(QT):
                    wait_alone(pool, s_qk_sb, 4 * t + kt + 1)
                    for g in range(NH):
                        nc.gpsimd.tensor_scalar(qmix[:, kt, :, g * RES:(g + 1) * RES],
                                                q[:, kt, :].rearrange("p (b i) -> p b i", i=RES),
                                                th1[:, kt, g:g + 1], SCALE, MUL, MUL).then_inc(s_qmix, 1)
                if not last:
                    rstd(t + 1)
                mixing_weights(t, first, 0)
                if not last:
                    pool.wait_ge(s_qk_mm, 4 * (t + 1))
                    x_low(t + 1)
                mixing_weights(t, first, 1)
            rounds(pool, step)
            residual_bias(PAIRS)


def kernel(**inputs):
    import concourse.bacc as bacc
    from concourse.bass_utils import run_bass_kernel_spmd

    a = {n.replace("L0_conv_", ""): np.asarray(v) for n, v in inputs.items()}

    def tiles(v):
        return v.reshape(-1, P).T

    def triple(f):
        return np.concatenate([tiles(a[f("q")]), tiles(a[f("k")]), tiles(a[f("v")])], axis=1)

    eye = np.eye(P, dtype=np.float32)
    c = np.arange(DIM)
    member = (c[:, None] // GC == np.arange(GROUPS)[None, :]).astype(np.float32)
    rows = np.abs(np.arange(2 * RES - 1) - (RES - 1))[None, :, None] * RES
    offs = rows + np.abs(np.arange(RES)[:, None, None] - np.arange(RES)[None, None, :])
    arrays = {
        "x": a["x"].reshape(BATCH, DIM, PIX),
        "wqkv": np.concatenate([a["qw"], a["kw"], a["vw"]], axis=0).T,
        "wp": a["pw"].T,
        "par": np.concatenate([triple(lambda n: n + "b"), triple(lambda n: n + "_s"), triple(lambda n: n + "_t"),
                               tiles(a["pb"]), tiles(a["p_s"]), tiles(a["p_t"]),
                               tiles(a["lvb"]), tiles(a["lv_s"]), tiles(a["lv_t"]),
                               a["lvw"].reshape(VT, P, 9).transpose(1, 0, 2).reshape(P, VT * 9)], axis=1),
        "th1": np.repeat(a["th1w"].T.reshape(QT, HR, NH), KD, axis=1).transpose(1, 0, 2),
        "ident": eye,
        "g_sum": (member * np.float32(1.0 / GC)).reshape(CT, P, GROUPS).transpose(1, 0, 2),
        "g_bc": member.reshape(CT, P, GROUPS).transpose(2, 0, 1),
        "small": np.concatenate([np.repeat(a["th1w"].T, RES, axis=0), np.repeat(a["th2w"].T, RES, axis=0),
                                 np.tile(np.eye(RES, dtype=np.float32), (NH, 1)),
                                 np.repeat(a["th1b"], RES)[:, None]], axis=1),
        "abx": a["ab"][:, offs].reshape(HP, WINDOW),
        "th2b": np.tile(np.repeat(a["th2b"], RES), RES).reshape(1, RES, HP),
    }
    nc = bacc.Bacc("TRN2", target_bir_lowering=False, num_devices=1, dynamic_dma_scratch_size=1024)
    feeds, aps = {}, {}
    for name, v in arrays.items():
        v = np.ascontiguousarray(v)
        feeds[f"in_{name}"] = v
        aps[name] = nc.dram_tensor(f"in_{name}", v.shape, mybir.dt.from_np(v.dtype), kind="ExternalInput").ap()
    out = nc.dram_tensor("out", (BATCH, DIM, PIX), mybir.dt.float32, kind="ExternalOutput").ap()
    build(nc, aps, out)
    r = run_bass_kernel_spmd(nc, [feeds], core_ids=[0])
    return r.results[0]["out"].reshape(BATCH, DIM, RES, RES)
```

```python
import numpy as np
import concourse.bass as bass
from concourse import mybir
from contextlib import ExitStack

BATCH, DIM, RES = 128, 384, 14
PIX = RES * RES
NH, KD, D = 8, 32, 128
DH = NH * D
GROUPS, GC = 32, DIM // 32
P = 128
PAIRS = BATCH // 2
CT = DIM // P
QT = NH * KD // P
VT = DH // P
COLS = 2 * PIX
HP = NH * RES
PITCH = RES + 1
HALF = RES // 2 * PITCH
HR = P // KD
VPAD = 32 * PITCH
ACC_ROWS = 2 * RES + 1
IMG = (RES + 1) * RES
ACC = ACC_ROWS * RES
WINDOW = (2 * RES - 1) * RES
BANK = 512
TAPS = [k for k in range(9) if k != 4]
SCALE = KD ** -0.5
EPS = 1e-5
NPAR = 3 * 12 + 3 * CT + 3 * VT + 9 * VT


def build(nc, A, out):
    f32, f32r = mybir.dt.float32, mybir.dt.float32r
    ALU, ACT = mybir.AluOpType, mybir.ActivationFunctionType
    MUL, ADD, SUB = ALU.mult, ALU.add, ALU.subtract

    with ExitStack() as ctx:
        def sb(name, shape, dt=f32):
            return ctx.enter_context(nc.sbuf_tensor(name, shape, dt))

        def sem(name):
            return ctx.enter_context(nc.semaphore(name))

        w_hi = sb("w_hi", [P, CT, 12 * P], f32r)
        w_lo = sb("w_lo", [P, CT, 12 * P], f32r)
        wp_hi = sb("wp_hi", [P, VT, DIM], f32r)
        wp_lo = sb("wp_lo", [P, VT, DIM], f32r)
        par = sb("par", [P, NPAR])
        th1 = sb("th1", [P, QT, NH])
        bias = sb("bias", [HP, WINDOW])
        kron2 = sb("kron2", [HP, NH, RES])
        ident = sb("ident", [P, P])
        g_sum = sb("g_sum", [P, CT, P])
        g_bc = sb("g_bc", [P, CT, P])
        small = sb("small", [HP, 2 * NH + RES + 1])
        abx = sb("abx", [HP, WINDOW])
        kron1 = sb("kron1", [HP, NH, RES])
        mhalf = sb("mhalf", [GROUPS, 2])
        xs = sb("xs", [P, CT, 2, PIX])
        bst = sb("bst", [P, 2 * CT, 6])
        mv = sb("mv", [P, 2 * CT, 2])
        mean_sq = sb("mean_sq", [P, 2 * CT])
        gs = sb("gs", [GROUPS, 2, 2])
        g_msq = sb("g_msq", [GROUPS, 2])
        g_var = sb("g_var", [GROUPS, 2])
        g_val = sb("g_val", [P, 2, 2])
        ab = sb("ab", [P, CT, 2, 2])
        x_hi = sb("x_hi", [P, CT, COLS], f32r)
        x_lo = sb("x_lo", [P, CT, COLS], f32r)
        q = sb("q", [P, QT, COLS])
        k = sb("k", [P, QT, COLS])
        qa = sb("qa", [P, 4 * RES * HP])
        probs = sb("probs", [P, 2, RES, 2 * HALF])
        nmax = sb("nmax", [HP, 2, RES])
        rowsum = sb("rowsum", [HP, 2, RES])
        rinv = sb("rinv", [HP, 2, RES])
        mixw = sb("mixw", [P, 2, RES, HP])
        vpad = sb("vpad", [P, VT, VPAD])
        vt = sb("vt", [P, 2, 2, DH])
        acc = sb("acc", [P, VT, ACC])
        o_hi = sb("o_hi", [P, VT, COLS], f32r)
        o_lo = sb("o_lo", [P, VT, COLS], f32r)
        res = sb("res", [P, CT, COLS])
        psA = ctx.enter_context(nc.psum_tensor("psA", [P, 2, BANK], f32))
        psL = ctx.enter_context(nc.psum_tensor("psL", [P, 2, BANK], f32))
        psM = ctx.enter_context(nc.psum_tensor("psM", [P, 2, BANK], f32))
        psP = ctx.enter_context(nc.psum_tensor("psP", [P, 2, BANK], f32))

        qmix = qa[:, :].rearrange("p (k b m) -> p k b m", k=QT, b=2 * RES)
        attn = qa[0:HALF, :].rearrange("p (i j g n) -> p i j g n", i=2, j=2, g=NH)
        stage_w = qa[:, 0:CT * 12 * P].rearrange("p (k m) -> p k m", k=CT)
        stage_p = acc[:, :, :].rearrange("p c n -> p (c n)")[:, 0:VT * DIM].rearrange("p (k m) -> p k m", k=VT)

        at = [0]

        def part(n, groups):
            v = par[:, at[0]:at[0] + n * groups]
            at[0] += n * groups
            return v.rearrange("p (a c) -> p a c", a=groups) if groups > 1 else v
        qkv_b, qkv_s, qkv_t = part(12, 1), part(12, 1), part(12, 1)
        p_b, p_s, p_t = part(CT, 1), part(CT, 1), part(CT, 1)
        l_b, l_s, l_t = part(VT, 1), part(VT, 1), part(VT, 1)
        taps = part(9, VT)
        th1r, th2r = small[:, 0:NH], small[:, NH:2 * NH]
        delta, th1b = small[:, 2 * NH:2 * NH + RES], small[:, 2 * NH + RES:2 * NH + RES + 1]

        x_pairs = A["x"].rearrange("(t i) (k p) n -> t k p i n", i=2, p=P)
        o_pairs = out.rearrange("(t i) (k p) n -> t k p i n", i=2, p=P)

        s_w, s_wp, s_par = sem("s_w"), sem("s_wp"), sem("s_par")
        s_x, s_res = sem("s_x"), sem("s_res")
        s_store = sem("s_store")
        s_kron1, s_kron2, s_c = sem("s_kron1"), sem("s_kron2"), sem("s_c")
        s_whi, s_prep, s_zero, s_biasmm = sem("s_whi"), sem("s_prep"), sem("s_zero"), sem("s_biasmm")
        s_ready = sem("s_ready")
        s_v_mm, s_qk_mm, s_proj_mm = sem("s_v_mm"), sem("s_qk_mm"), sem("s_proj_mm")
        s_logit_mm, s_vt_mm, s_mix_mm, s_av_mm = sem("s_logit_mm"), sem("s_vt_mm"), sem("s_mix_mm"), sem("s_av_mm")
        s_gsum_mm, s_gbc_mm = sem("s_gsum_mm"), sem("s_gbc_mm")
        s_v_sb, s_conv0, s_qk_sb, s_exp = sem("s_v_sb"), sem("s_conv0"), sem("s_qk_sb"), sem("s_exp")
        s_xhi, s_vt_sb, s_mix_sb, s_relu = sem("s_xhi"), sem("s_vt_sb"), sem("s_mix_sb"), sem("s_relu")
        s_conv, s_score, s_rinv = sem("s_conv"), sem("s_score"), sem("s_rinv")
        s_out, s_add, s_olo = sem("s_out"), sem("s_add"), sem("s_olo")
        s_bst, s_mv, s_msq, s_stat = sem("s_bst"), sem("s_mv"), sem("s_msq"), sem("s_stat")
        s_gs, s_gmsq, s_gvar, s_gval, s_ab, s_xn = (sem(n) for n in ("s_gs", "s_gmsq", "s_gvar", "s_gval", "s_ab", "s_xn"))
        s_qmix, s_resb, s_rstd, s_xlo, s_mixw = sem("s_qmix"), sem("s_resb"), sem("s_rstd"), sem("s_xlo"), sem("s_mixw")

        block = ctx.enter_context(nc.Block())
        N_PAR_DMA = 9

        def keys(img, b):
            return probs[0:HP, img, b, :].rearrange("p (r w) -> p r w", w=PITCH)[:, :, 0:RES]

        def group(b):
            return b // 4

        USES = [("vt", 0), ("mix", 0), ("vt", 1), ("mix", 1), ("vt", 2), ("mix", 2), ("vt", 3), ("mix", 3),
                ("mix", 4), ("mix", 5), ("mix", 6)]

        def mix_bank(use):
            return (psM if use % 4 < 2 else psL)[0:HALF, use % 2, :]

        def t_has_next(t):
            return not isinstance(t, int) or t < PAIRS - 1

        def wait_alone(eng, semaphore, value):
            eng.wait_ge(semaphore, value)
            eng.nop(nofuse=True)

        def rounds(eng, step):
            step(0, True, False)
            with eng.Fori(1, PAIRS - 1) as t:
                step(t, False, False)
            step(PAIRS - 1, False, True)

        @block.sync
        def _(sp):
            sp.dma_start(stage_w, A["wqkv"].rearrange("(k p) m -> p k m", p=P)).then_inc(s_w, 16)
            for kt in range(CT):
                sp.dma_start(xs[:, kt, :, :], x_pairs[0, kt]).then_inc(s_x, 16)
            sp.dma_start(stage_p, A["wp"].rearrange("(k p) m -> p k m", p=P)).then_inc(s_wp, 16)
            sp.wait_ge(s_zero, 1)
            for dst, src in ((par[:, :], A["par"]), (th1[:, :, :], A["th1"]), (ident[:, :], A["ident"]),
                             (g_sum[:, :, :], A["g_sum"]), (g_bc[:, :, :], A["g_bc"]), (small[:, :], A["small"]),
                             (abx[:, :], A["abx"]),
                             (mixw[HP:HP + 1, 0, :, :], A["th2b"]), (mixw[HP:HP + 1, 1, :, :], A["th2b"])):
                sp.dma_start(dst, src).then_inc(s_par, 16)

            def residual(t):
                for kt in range(CT):
                    sp.dma_start(res[:, kt, :].rearrange("p (i n) -> p i n", i=2),
                                 x_pairs[t - 1, kt]).then_inc(s_res, 16)

            def store(t):
                for kt in range(CT):
                    sp.wait_ge(s_out, 3 * (t - 1) + kt + 2)
                    sp.dma_start(o_pairs[t - 1, kt],
                                 res[:, kt, :].rearrange("p (i n) -> p i n", i=2)).then_inc(s_store, 16)
                wait_alone(sp, s_store, 48 * t)

            def step(t, first, last):
                if not first:
                    residual(t)
                if not last:
                    sp.wait_ge(s_xhi, t + 1)
                    sp.wait_ge(s_xlo, t + 1)
                    for kt in range(CT):
                        sp.dma_start(xs[:, kt, :, :], x_pairs[t + 1, kt]).then_inc(s_x, 16)
                if not first:
                    store(t)
            rounds(sp, step)
            residual(PAIRS)
            store(PAIRS)

        @block.tensor
        def _(pe):
            def split3(dst, terms, hi, lo, m0, rhi, rlo):
                for c in range(terms):
                    for n, (w, r) in enumerate(((lo, rhi), (hi, rlo), (hi, rhi))):
                        last = nc.tensor.matmul(dst, w[:, c, m0:m0 + P], r[:, c, :], start=(c == 0 and n == 0),
                                                stop=(c == terms - 1 and n == 2))
                return last

            def group_sums(p):
                pe.wait_ge(s_stat, p + 1)
                for kt in range(CT):
                    last = nc.tensor.matmul(psP[:, 1, 0:4], g_sum[:, kt, :],
                                            mv[:, 2 * kt:2 * kt + 2, :].rearrange("p i s -> p (i s)"),
                                            start=(kt == 0), stop=(kt == CT - 1))
                last.then_inc(s_gsum_mm, 1)

            def group_broadcast(p):
                pe.wait_ge(s_gval, p + 1)
                for kt in range(CT):
                    last = nc.tensor.matmul(psP[:, 1, 8 + 4 * kt:12 + 4 * kt], g_bc[:, kt, :],
                                            g_val[:, :, :].rearrange("p i s -> p (i s)"), start=True, stop=True)
                last.then_inc(s_gbc_mm, 1)

            def project(t, m):
                if m == 0:
                    pe.wait_ge(s_relu, 8 * t)
                    pe.wait_ge(s_olo, 8 * t)
                    pe.wait_ge(s_out, 3 * (t - 1) + 1)
                elif m == 1:
                    pe.wait_ge(s_ab, t + 2 if t_has_next(t) else PAIRS)
                else:
                    pe.wait_ge(s_out, 3 * (t - 1) + 2)
                split3(psP[:, m % 2, 0:COLS], VT, wp_hi, wp_lo, m * P, o_hi, o_lo).then_inc(s_proj_mm, 1)

            pe.wait_ge(s_kron1, 1)
            nc.tensor.matmul(psP[0:HP, 0, 0:WINDOW], kron1[:, :, :].rearrange("p g i -> p (g i)"), abx[:, :],
                             start=True, stop=True).then_inc(s_biasmm, 1)
            group_sums(0)
            group_broadcast(0)
            pe.wait_ge(s_prep, 2)

            def step(t, first, last):
                pe.wait_ge(s_xhi, t + 1)
                pe.wait_ge(s_xlo, t + 1)
                for m in range(4):
                    if m >= 2:
                        pe.wait_ge(s_qk_sb, 4 * t + m - 1)
                    elif not first:
                        pe.wait_ge(s_add, 8 * t - 1 + m)
                    split3(psA[:, m % 2, 0:COLS], CT, w_hi, w_lo, m * P, x_hi, x_lo).then_inc(s_qk_mm, 1)
                for m in range(VT):
                    if m >= 2:
                        pe.wait_ge(s_v_sb, VT * t + m - 1)
                    else:
                        pe.wait_ge(s_qk_sb, 4 * t + 3 + m)
                    split3(psA[:, m % 2, 0:COLS], CT, w_hi, w_lo, (4 + m) * P, x_hi, x_lo).then_inc(s_v_mm, 1)
                if not last:
                    group_sums(t + 1)
                pe.wait_ge(s_qk_sb, 4 * (t + 1))
                pe.wait_ge(s_qmix, 16 * (t + 1))
                for n in range(RES):
                    img, b0 = n // 7, 2 * (n % 7)
                    if n >= 2:
                        pe.wait_ge(s_score, 28 * t + 2 * n - 2)
                    elif not first:
                        pe.wait_ge(s_mix_sb, 14 * (t - 1) + 12 + n)
                    for b in (b0, b0 + 1):
                        for kt in range(QT):
                            mm = nc.tensor.matmul(psL[0:HP, n % 2, (b - b0) * PIX:(b - b0 + 1) * PIX],
                                                  qmix[:, kt, img * RES + b, :], k[:, kt, img * PIX:(img + 1) * PIX],
                                                  start=(kt == 0), stop=(kt == QT - 1))
                    mm.then_inc(s_logit_mm, 1)
                    if n == 6 and not last:
                        group_broadcast(t + 1)
                if not first:
                    project(t, 0)
                def bank_free(use):
                    ago, tt = use - 4, t
                    if use in (2, 3):
                        pe.wait_ge(s_score, 28 * t + 22 + 2 * use)
                        return
                    if use < 2:
                        if first:
                            return
                        ago, tt = use + 20, t - 1
                    i, (what, n) = ago // 11, USES[ago % 11]
                    if what == "vt":
                        pe.wait_ge(s_vt_sb, 8 * tt + 4 * i + n + 1)
                    else:
                        pe.wait_ge(s_mix_sb, 14 * tt + 7 * i + n + 1)

                for use in range(22):
                    img, (what, n) = use // 11, USES[use % 11]
                    bank_free(use)
                    if what == "vt":
                        jc, cg = divmod(n, 2)
                        for c in range(4):
                            at_ = PITCH + 1 + img * PITCH * PITCH + jc * HALF
                            mm = nc.tensor.transpose(mix_bank(use)[:, c * P:(c + 1) * P],
                                                     vpad[:, 4 * cg + c, at_:at_ + HALF], ident[:, :])
                        mm.then_inc(s_vt_mm, 1)
                    else:
                        pe.wait_ge(s_exp, 28 * t + 14 * img + 2 * n + 2)
                        pe.wait_ge(s_mixw, 8 * t + 4 * img + group(2 * n + 1) + 1)
                        bank = mix_bank(use)[:, 0:4 * HP].rearrange("p (j g b i) -> p j g b i", j=2, g=NH, b=2)
                        for jc in range(2):
                            for b in range(2):
                                mm = nc.tensor.matmul(bank[:, jc, :, b, :],
                                                      probs[0:HP + 1, img, 2 * n + b, jc * HALF:(jc + 1) * HALF],
                                                      mixw[0:HP + 1, img, 2 * n + b, :].rearrange("p (g i) -> p g i", g=NH),
                                                      start=True, stop=True)
                        mm.then_inc(s_mix_mm, 1)
                if not first:
                    project(t, 1)
                    project(t, 2)
                for img in range(2):
                    pe.wait_ge(s_vt_sb, 8 * t + 4 * img + 4)
                    pe.wait_ge(s_mix_sb, 14 * t + 7 * img + 7)
                    for n in range(4):
                        u = 4 * img + n
                        if u < 2:
                            pe.wait_ge(s_v_sb, VT * t + 7 + u)
                        else:
                            pe.wait_ge(s_add, 8 * t + u - 1)
                        for e in range(2):
                            g = 2 * n + e
                            for jc in range(2):
                                mm = nc.tensor.matmul(psA[:, u % 2, e * PIX:(e + 1) * PIX],
                                                      vt[0:HALF, img, jc, g * D:(g + 1) * D], attn[:, img, jc, g, :],
                                                      start=(jc == 0), stop=(jc == 1))
                        mm.then_inc(s_av_mm, 1)
            rounds(pe, step)
            for m in range(CT):
                project(PAIRS, m)

        @block.scalar
        def _(act):
            act.wait_ge(s_w, 16)
            nc.scalar.copy(w_hi[:, :, :], stage_w).then_inc(s_whi, 1)
            act.wait_ge(s_wp, 16)
            nc.scalar.copy(wp_hi[:, :, :], stage_p).then_inc(s_whi, 1)

            def x_high(p):
                act.wait_ge(s_xn, 6 * (p + 1))
                nc.scalar.copy(x_hi[:, :, :], xs[:, :, :, :].rearrange("p k i n -> p k (i n)")).then_inc(s_xhi, 1)
            x_high(0)

            def conv_centre(t, c):
                act.wait_ge(s_v_sb, VT * t + c + 1)
                src = vpad[:, c, PITCH + 1:PITCH + 1 + ACC_ROWS * PITCH].rearrange("p (r w) -> p r w", w=PITCH)
                nc.scalar.activation(acc[:, c, :].rearrange("p (r w) -> p r w", w=RES), src[:, :, 0:RES],
                                     ACT.Identity, bias=l_t[:, c:c + 1], scale=taps[:, c, 4:5]).then_inc(s_conv0, 1)

            def relu(t, img, n):
                act.wait_ge(s_add, 8 * t + 4 * img + n + 1)
                nc.scalar.activation(o_hi[:, 2 * n:2 * n + 2, img * PIX:(img + 1) * PIX],
                                     acc[:, 2 * n:2 * n + 2, img * IMG:img * IMG + PIX], ACT.Relu).then_inc(s_relu, 1)

            act.wait_ge(s_ready, 1)

            def step(t, first, last):
                for m in range(4):
                    act.wait_ge(s_qk_mm, 4 * t + m + 1)
                    if m == 0 and not first:
                        act.wait_ge(s_qmix, 16 * t)
                    if m == 2 and not first:
                        act.wait_ge(s_logit_mm, 14 * t)
                    dst = (q if m < 2 else k)[:, m % 2, :]
                    nc.scalar.activation(dst, psA[:, m % 2, 0:COLS], ACT.Identity, bias=qkv_t[:, m:m + 1],
                                         scale=qkv_s[:, m:m + 1]).then_inc(s_qk_sb, 1)
                if not first:
                    act.wait_ge(s_vt_mm, 8 * t)
                    act.wait_ge(s_conv, 64 * t)
                    act.wait_ge(s_olo, 8 * t)
                else:
                    act.wait_ge(s_prep, 2)
                for m in range(VT):
                    act.wait_ge(s_v_mm, VT * t + m + 1)
                    at_ = PITCH + 1
                    dst = vpad[:, m, at_:at_ + 2 * PITCH * PITCH].rearrange("p (i r w) -> p i r w", i=2, w=PITCH)
                    nc.scalar.activation(dst[:, :, 0:RES, 0:RES],
                                         psA[:, m % 2, 0:COLS].rearrange("p (i r w) -> p i r w", i=2, w=RES),
                                         ACT.Identity, bias=qkv_t[:, 4 + m:5 + m],
                                         scale=qkv_s[:, 4 + m:5 + m]).then_inc(s_v_sb, 1)
                    if m:
                        conv_centre(t, m - 1)
                conv_centre(t, VT - 1)
                if not first:
                    act.wait_ge(s_rinv, 2 * t)
                for n in range(2 * RES):
                    img, b = divmod(n, RES)
                    act.wait_ge(s_score, 28 * t + n + 1)
                    row = keys(img, b)
                    nc.scalar.activation(row, row, ACT.Exp,
                                         bias=nmax[:, img, b:b + 1], scale=-1.0,
                                         accum_out=rowsum[:, img, b:b + 1]).then_inc(s_exp, 1)
                for use in range(22):
                    img, (what, n) = use // 11, USES[use % 11]
                    if what == "vt":
                        jc, cg = divmod(n, 2)
                        act.wait_ge(s_vt_mm, 8 * t + 4 * img + n + 1)
                        if use == 0 and not first:
                            act.wait_ge(s_av_mm, 8 * t)
                        nc.scalar.copy(vt[0:HALF, img, jc, cg * BANK:(cg + 1) * BANK],
                                       mix_bank(use)).then_inc(s_vt_sb, 1)
                    else:
                        act.wait_ge(s_mix_mm, 14 * t + 7 * img + n + 1)
                        src = mix_bank(use)[:, 0:4 * HP].rearrange("p (j g m) -> p j g m", j=2, g=NH)
                        nc.scalar.copy(attn[:, img, :, :, 2 * n * RES:(2 * n + 2) * RES], src).then_inc(s_mix_sb, 1)
                if not last:
                    act.wait_ge(s_v_mm, VT * (t + 1))
                    x_high(t + 1)
                if not first:
                    act.wait_ge(s_proj_mm, 3 * t)
                for img in range(2):
                    for n in range(4):
                        relu(t, img, n)
            rounds(act, step)

        @block.vector
        def _(dve):
            nc.vector.memset(mixw[:, :, :, :], 0.0).then_inc(s_zero, 1)
            nc.vector.memset(probs[:, :, :, :], 1.0)
            nc.vector.memset(vpad[:, :, :], 0.0)
            nc.vector.memset(mhalf[:, :], -0.5)
            nc.vector.memset(g_val[:, :, :], 0.0)
            dve.wait_ge(s_par, 16 * N_PAR_DMA)
            for dst, src, signal in ((kron2, th2r, s_kron2), (kron1, th1r, s_kron1)):
                nc.vector.tensor_tensor(dst[:, :, :], src.unsqueeze(2).broadcast_to([HP, NH, RES]),
                                        delta.unsqueeze(1).broadcast_to([HP, NH, RES]), MUL).then_inc(signal, 1)
            nc.vector.tensor_tensor(qkv_b, qkv_b, qkv_s, MUL)
            nc.vector.tensor_tensor(p_b, p_b, p_s, MUL)
            nc.vector.tensor_tensor(l_b, l_b, l_s, MUL)
            nc.vector.tensor_tensor(taps, taps, l_s.unsqueeze(2).broadcast_to([P, VT, 9]), MUL).then_inc(s_c, 1)
            dve.wait_ge(s_c, 1)
            nc.vector.tensor_tensor(qkv_t, qkv_t, qkv_b, ADD)
            nc.vector.tensor_tensor(p_t, p_t, p_b, ADD)
            nc.vector.tensor_tensor(l_t, l_t, l_b, ADD).then_inc(s_ready, 1)

            def stats(p):
                dve.wait_ge(s_x, 48 * (p + 1))
                for n in range(2 * CT):
                    nc.vector.bn_stats(bst[:, n, :], xs[:, n // 2, n % 2, :]).then_inc(s_bst, 1)
                wait_alone(dve, s_bst, 6 * (p + 1))
                for n in range(2 * CT):
                    nc.vector.bn_aggr(mv[:, n, :], bst[:, n, :]).then_inc(s_mv, 1)
                dve.wait_ge(s_mv, 6 * (p + 1))
                nc.vector.tensor_tensor(mean_sq[:, :], mv[:, :, 0], mv[:, :, 0], MUL).then_inc(s_msq, 1)
                dve.wait_ge(s_msq, p + 1)
                nc.vector.tensor_tensor(mv[:, :, 1], mv[:, :, 1], mean_sq[:, :], ADD).then_inc(s_stat, 1)

            def group_variance(p, n):
                if n == 0:
                    dve.wait_ge(s_gsum_mm, p + 1)
                    nc.vector.tensor_copy(gs[:, :, :].rearrange("p i s -> p (i s)"), psP[0:GROUPS, 1, 0:4]).then_inc(s_gs, 1)
                elif n == 1:
                    dve.wait_ge(s_gs, p + 1)
                    nc.vector.tensor_tensor(g_msq[:, :], gs[:, :, 0], gs[:, :, 0], MUL).then_inc(s_gmsq, 1)
                else:
                    dve.wait_ge(s_gmsq, p + 1)
                    nc.vector.scalar_tensor_tensor(g_var[:, :], gs[:, :, 1], EPS, g_msq[:, :], ADD, SUB).then_inc(s_gvar, 1)

            def group_values(p):
                dve.wait_ge(s_rstd, p + 1)
                nc.vector.scalar_tensor_tensor(g_val[0:GROUPS, :, 1], gs[:, :, 0], -1.0, g_val[0:GROUPS, :, 0],
                                               MUL, MUL).then_inc(s_gval, 1)

            def channel_values(p):
                dve.wait_ge(s_gbc_mm, p + 1)
                nc.vector.tensor_copy(ab[:, :, :, :].rearrange("p k i s -> p (k i s)"), psP[:, 1, 8:20]).then_inc(s_ab, 1)

            def normalise(p, n):
                kt, i = divmod(n, 2)
                dve.wait_ge(s_ab, p + 1)
                nc.vector.tensor_scalar(xs[:, kt, i, :], xs[:, kt, i, :], ab[:, kt, i, 0:1], ab[:, kt, i, 1:2],
                                        MUL, ADD).then_inc(s_xn, 1)

            stats(0)
            for n in range(3):
                group_variance(0, n)
            group_values(0)
            channel_values(0)
            for n in range(6):
                normalise(0, n)
            dve.wait_ge(s_whi, 1)
            nc.vector.tensor_tensor(w_lo[:, :, :], stage_w, w_hi[:, :, :].bitcast(f32), SUB).then_inc(s_prep, 1)
            dve.wait_ge(s_whi, 2)
            nc.vector.tensor_tensor(wp_lo[:, :, :], stage_p, wp_hi[:, :, :].bitcast(f32), SUB).then_inc(s_prep, 1)
            dve.wait_ge(s_biasmm, 1)
            nc.vector.tensor_scalar(bias[:, :], psP[0:HP, 0, 0:WINDOW], th1b, None, ADD).then_inc(s_out, 1)

            def conv(t, first, c0, n):
                tap, e = divmod(n, 2)
                c = c0 + e
                if tap == 0:
                    dve.wait_ge(s_conv0, VT * t + c + 1)
                else:
                    dve.wait_ge(s_conv, 64 * t + 8 * c0 + 2 * (tap - 1) + e + 1)
                dy, dx = divmod(TAPS[tap], 3)
                at_ = dy * PITCH + dx
                src = vpad[:, c, at_:at_ + ACC_ROWS * PITCH].rearrange("p (r w) -> p r w", w=PITCH)[:, :, 0:RES]
                a = acc[:, c, :].rearrange("p (r w) -> p r w", w=RES)
                nc.vector.scalar_tensor_tensor(a, src, taps[:, c, TAPS[tap]:TAPS[tap] + 1], a, MUL, ADD).then_inc(s_conv, 1)

            def project_out(t, m):
                dve.wait_ge(s_resb, 3 * (t - 1) + m + 1)
                dve.wait_ge(s_proj_mm, 3 * (t - 1) + m + 1)
                nc.vector.scalar_tensor_tensor(res[:, m, :], psP[:, m % 2, 0:COLS], p_s[:, m:m + 1], res[:, m, :],
                                               MUL, ADD).then_inc(s_out, 1)

            def step(t, first, last):
                todo = iter([(c, n) for c in range(0, VT, 2) for n in range(16)])

                def convs(count):
                    for _ in range(count):
                        nxt = next(todo, None)
                        if nxt:
                            conv(t, first, *nxt)

                if not last:
                    stats(t + 1)
                convs(16)
                if first:
                    dve.wait_ge(s_out, 1)
                if not first:
                    dve.wait_ge(s_mix_mm, 14 * t)
                for n in range(RES):
                    wait_alone(dve, s_logit_mm, 14 * t + n + 1)
                    for r in (2 * n, 2 * n + 1):
                        img, b = divmod(r, RES)
                        at_ = (RES - 1 - b) * RES
                        nc.vector.tensor_tensor_reduce(
                            out=keys(img, b),
                            in0=psL[0:HP, n % 2, (r % 2) * PIX:(r % 2 + 1) * PIX].rearrange("p (r w) -> p r w", w=RES),
                            in1=bias[:, at_:at_ + PIX].rearrange("p (r w) -> p r w", w=RES), scale=-1.0, scalar=3.4028234e38, op0=ADD, op1=ALU.min,
                            accum_out=nmax[:, img, b:b + 1]).then_inc(s_score, 1)
                    if n < 3 and not last:
                        group_variance(t + 1, n)
                    elif n == 4 and not last:
                        group_values(t + 1)
                    elif n == 8 and not last:
                        channel_values(t + 1)
                    elif n == 9:
                        dve.wait_ge(s_exp, 28 * t + 14)
                        if not first:
                            dve.wait_ge(s_mixw, 8 * t)
                        nc.vector.reciprocal(rinv[:, 0, :], rowsum[:, 0, :]).then_inc(s_rinv, 1)
                    if n >= 10 and not last:
                        normalise(t + 1, n - 10)
                    convs(1)
                convs(2)
                dve.wait_ge(s_exp, 28 * t + 28)
                nc.vector.reciprocal(rinv[:, 1, :], rowsum[:, 1, :]).then_inc(s_rinv, 1)
                if not last:
                    normalise(t + 1, 4)
                    normalise(t + 1, 5)
                convs(4)
                if not first:
                    project_out(t, 0)
                convs(64)
                if not first:
                    project_out(t, 1)
                    project_out(t, 2)
                if not first:
                    dve.wait_ge(s_proj_mm, 3 * t)

                def low(u):
                    img, n = divmod(u, 4)
                    dve.wait_ge(s_relu, 8 * t + u + 1)
                    a = acc[:, 2 * n:2 * n + 2, img * IMG:img * IMG + PIX]
                    sl = (slice(None), slice(2 * n, 2 * n + 2), slice(img * PIX, (img + 1) * PIX))
                    nc.vector.scalar_tensor_tensor(o_lo[sl], a, 0.0, o_hi[sl].bitcast(f32), ALU.max, SUB).then_inc(s_olo, 1)

                for u in range(8):
                    img, n = divmod(u, 4)
                    dve.wait_ge(s_conv, 64 * t + 16 * (n + 1))
                    dve.wait_ge(s_av_mm, 8 * t + u + 1)
                    a = acc[:, 2 * n:2 * n + 2, img * IMG:img * IMG + PIX]
                    nc.vector.tensor_tensor(a, psA[:, n % 2, 0:COLS].rearrange("p (c n) -> p c n", c=2), a,
                                            ADD).then_inc(s_add, 1)
                    if u:
                        low(u - 1)
                low(7)
            rounds(dve, step)
            for m in range(CT):
                project_out(PAIRS, m)

        @block.gpsimd
        def _(pool):
            pool.wait_ge(s_ready, 1)

            def rstd(p):
                pool.wait_ge(s_gvar, p + 1)
                nc.gpsimd.tensor_tensor(g_val[0:GROUPS, :, 0], g_var[:, :], mhalf[:, :], ALU.pow).then_inc(s_rstd, 1)

            def x_low(p):
                pool.wait_ge(s_xhi, p + 1)
                nc.gpsimd.tensor_tensor(x_lo[:, :, :], xs[:, :, :, :].rearrange("p k i n -> p k (i n)"),
                                        x_hi[:, :, :].bitcast(f32), SUB).then_inc(s_xlo, 1)

            def residual_bias(t):
                wait_alone(pool, s_res, 48 * t)
                for m in range(CT):
                    nc.gpsimd.tensor_scalar(res[:, m, :], res[:, m, :], p_t[:, m:m + 1], 1.0, ADD, MUL).then_inc(s_resb, 1)

            def mixing_weights(t, first, img):
                if not first:
                    pool.wait_ge(s_mix_mm, 14 * (t - 1) + 7 * (img + 1))
                pool.wait_ge(s_rinv, 2 * t + img + 1)
                for b0 in range(0, RES, 4):
                    nb = min(4, RES - b0)
                    k2 = kron2[:, :, :].rearrange("p g i -> p (g i)").unsqueeze(1).broadcast_to([HP, nb, HP])
                    nc.gpsimd.tensor_tensor(mixw[0:HP, img, b0:b0 + nb, :], k2,
                                            rinv[:, img, b0:b0 + nb].unsqueeze(2).broadcast_to([HP, nb, HP]),
                                            MUL).then_inc(s_mixw, 1)

            rstd(0)
            x_low(0)
            pool.wait_ge(s_prep, 1)

            def step(t, first, last):
                if not first:
                    pool.wait_ge(s_av_mm, 8 * t)
                for kt in range(QT):
                    wait_alone(pool, s_qk_sb, 4 * t + kt + 1)
                    for g in range(NH):
                        nc.gpsimd.tensor_scalar(qmix[:, kt, :, g * RES:(g + 1) * RES],
                                                q[:, kt, :].rearrange("p (b i) -> p b i", i=RES),
                                                th1[:, kt, g:g + 1], SCALE, MUL, MUL).then_inc(s_qmix, 1)
                if not last:
                    rstd(t + 1)
                if not first:
                    residual_bias(t)
                mixing_weights(t, first, 0)
                mixing_weights(t, first, 1)
                if not last:
                    pool.wait_ge(s_v_mm, VT * (t + 1))
                    x_low(t + 1)
            rounds(pool, step)
            residual_bias(PAIRS)


def kernel(**inputs):
    import concourse.bacc as bacc
    from concourse.bass_utils import run_bass_kernel_spmd

    a = {n.replace("L0_conv_", ""): np.asarray(v) for n, v in inputs.items()}

    def tiles(v):
        return v.reshape(-1, P).T

    def triple(f):
        return np.concatenate([tiles(a[f("q")]), tiles(a[f("k")]), tiles(a[f("v")])], axis=1)

    eye = np.eye(P, dtype=np.float32)
    c = np.arange(DIM)
    member = (c[:, None] // GC == np.arange(P)[None, :]).astype(np.float32)
    rows = np.abs(np.arange(2 * RES - 1) - (RES - 1))[None, :, None] * RES
    offs = rows + np.abs(np.arange(RES)[:, None, None] - np.arange(RES)[None, None, :])
    arrays = {
        "x": a["x"].reshape(BATCH, DIM, PIX),
        "wqkv": np.concatenate([a["qw"], a["kw"], a["vw"]], axis=0).T,
        "wp": a["pw"].T,
        "par": np.concatenate([triple(lambda n: n + "b"), triple(lambda n: n + "_s"), triple(lambda n: n + "_t"),
                               tiles(a["pb"]), tiles(a["p_s"]), tiles(a["p_t"]),
                               tiles(a["lvb"]), tiles(a["lv_s"]), tiles(a["lv_t"]),
                               a["lvw"].reshape(VT, P, 9).transpose(1, 0, 2).reshape(P, VT * 9)], axis=1),
        "th1": np.repeat(a["th1w"].T.reshape(QT, HR, NH), KD, axis=1).transpose(1, 0, 2),
        "ident": eye,
        "g_sum": (member * np.float32(1.0 / GC)).reshape(CT, P, P).transpose(1, 0, 2),
        "g_bc": member.reshape(CT, P, P).transpose(2, 0, 1),
        "small": np.concatenate([np.repeat(a["th1w"].T, RES, axis=0), np.repeat(a["th2w"].T, RES, axis=0),
                                 np.tile(np.eye(RES, dtype=np.float32), (NH, 1)),
                                 np.repeat(a["th1b"], RES)[:, None]], axis=1),
        "abx": a["ab"][:, offs].reshape(HP, WINDOW),
        "th2b": np.tile(np.repeat(a["th2b"], RES), RES).reshape(1, RES, HP),
    }
    nc = bacc.Bacc("TRN2", target_bir_lowering=False, num_devices=1, dynamic_dma_scratch_size=1024)
    feeds, aps = {}, {}
    for name, v in arrays.items():
        v = np.ascontiguousarray(v)
        feeds[f"in_{name}"] = v
        aps[name] = nc.dram_tensor(f"in_{name}", v.shape, mybir.dt.from_np(v.dtype), kind="ExternalInput").ap()
    out = nc.dram_tensor("out", (BATCH, DIM, PIX), mybir.dt.float32, kind="ExternalOutput").ap()
    build(nc, aps, out)
    r = run_bass_kernel_spmd(nc, [feeds], core_ids=[0])
    return r.results[0]["out"].reshape(BATCH, DIM, RES, RES)
```

```python
import numpy as np
import concourse.bass as bass
from concourse import mybir
from contextlib import ExitStack

BATCH, DIM, RES = 128, 384, 14
PIX = RES * RES
NH, KD, D = 8, 32, 128
DH = NH * D
GROUPS, GC = 32, DIM // 32
P = 128
PAIRS = BATCH // 2
CT = DIM // P
QT = NH * KD // P
VT = DH // P
COLS = 2 * PIX
HP = NH * RES
PITCH = RES + 1
HALF = RES // 2 * PITCH
HR = P // KD
VPAD = 32 * PITCH
ACC_ROWS = 2 * RES + 1
IMG = (RES + 1) * RES
ACC = ACC_ROWS * RES
WINDOW = (2 * RES - 1) * RES
BANK = 512
TAPS = [k for k in range(9) if k != 4]
SCALE = KD ** -0.5
EPS = 1e-5
NPAR = 3 * 12 + 3 * CT + 3 * VT + 9 * VT


def build(nc, A, out):
    f32, f32r = mybir.dt.float32, mybir.dt.float32r
    ALU, ACT = mybir.AluOpType, mybir.ActivationFunctionType
    MUL, ADD, SUB = ALU.mult, ALU.add, ALU.subtract

    with ExitStack() as ctx:
        def sb(name, shape, dt=f32):
            return ctx.enter_context(nc.sbuf_tensor(name, shape, dt))

        def over(name, shape, skip=0):
            with nc.sbuf_tensor(f"{name}_skip", [P, max(skip, 1)], f32) if skip else ExitStack():
                with nc.sbuf_tensor(name, shape, f32r) as tensor:
                    return tensor

        def sem(name):
            return ctx.enter_context(nc.semaphore(name))

        w_hi = sb("w_hi", [P, CT, 12 * P], f32r)
        w_lo = sb("w_lo", [P, CT, 12 * P], f32r)
        wp_hi = sb("wp_hi", [P, VT, DIM], f32r)
        wp_lo = sb("wp_lo", [P, VT, DIM], f32r)
        par = sb("par", [P, NPAR])
        th1 = sb("th1", [P, QT, NH])
        bias = sb("bias", [HP, WINDOW])
        kron2 = sb("kron2", [HP, NH, RES])
        ident = sb("ident", [P, P])
        g_sum = sb("g_sum", [P, GROUPS])
        g_bc = sb("g_bc", [GROUPS, P])
        small = sb("small", [HP, 2 * NH + RES + 1])
        mhalf = sb("mhalf", [GROUPS, 2])
        xs = sb("xs", [P, 2, CT, PIX])
        bst = sb("bst", [P, 2, 2, 6])
        mv = sb("mv", [P, 2, 2])
        mean_sq = sb("mean_sq", [P, 2])
        gs = sb("gs", [GROUPS, 2, 2])
        g_msq = sb("g_msq", [GROUPS, 2])
        g_var = sb("g_var", [GROUPS, 2])
        g_val = sb("g_val", [GROUPS, 2, 2])
        ab = sb("ab", [P, 2, 2])
        x_hi = sb("x_hi", [P, 2, CT, PIX], f32r)
        x_lo = sb("x_lo", [P, 2, CT, PIX], f32r)
        q = sb("q", [P, QT, COLS])
        k_hi = sb("k_hi", [P, QT, COLS], f32r)
        k_lo = over("k_lo", [P, QT, COLS])
        k = sb("k", [P, QT, COLS])
        q_hi = over("q_hi", [P, 2 * RES, QT, HP])
        qa = sb("qa", [P, 4 * RES * HP])
        probs = sb("probs", [P, 2, RES, 2 * HALF])
        nmax = sb("nmax", [HP, 2, RES])
        rowsum = sb("rowsum", [HP, 2, RES])
        rinv = sb("rinv", [HP, 2, RES])
        mixw = sb("mixw", [P, 2, RES, HP])
        vpad = sb("vpad", [P, VT, VPAD])
        o_hi = sb("o_hi", [P, VT, COLS], f32r)
        o_lo = over("o_lo", [P, VT, COLS])
        stage_wp = sb("stage_wp", [P, VT * COLS])
        q_lo = over("q_lo", [P, 2 * RES, QT, HP], VT // 2 * ACC)
        shared = sb("shared", [P, VT * ACC + 4 * DH + CT * COLS])
        psA = ctx.enter_context(nc.psum_tensor("psA", [P, 2, BANK], f32))
        psL = ctx.enter_context(nc.psum_tensor("psL", [P, 2, BANK], f32))
        psM = ctx.enter_context(nc.psum_tensor("psM", [P, 2, BANK], f32))
        psP = ctx.enter_context(nc.psum_tensor("psP", [P, 2, BANK], f32))

        vt_at, res_at = VT * ACC, VT * ACC + 4 * DH
        acc = shared[:, 0:vt_at].rearrange("p (c n) -> p c n", c=VT)
        vt = shared[:, vt_at:res_at].rearrange("p (i j n) -> p i j n", i=2, j=2)
        res = shared[:, res_at:].rearrange("p (i k n) -> p i k n", i=2, k=CT)
        abx = shared[0:HP, vt_at:vt_at + WINDOW]
        kron1 = shared[0:HP, vt_at + WINDOW:vt_at + WINDOW + HP].rearrange("p (g i) -> p g i", g=NH)
        attn = qa[0:HALF, :].rearrange("p (i j g n) -> p i j g n", i=2, j=2, g=NH)
        stage_w = qa[:, 0:CT * 12 * P].rearrange("p (k m) -> p k m", k=CT)
        stage_p = stage_wp[:, 0:VT * DIM].rearrange("p (k m) -> p k m", k=VT)

        at = [0]

        def part(n, groups):
            v = par[:, at[0]:at[0] + n * groups]
            at[0] += n * groups
            return v.rearrange("p (a c) -> p a c", a=groups) if groups > 1 else v
        qkv_b, qkv_s, qkv_t = part(12, 1), part(12, 1), part(12, 1)
        p_b, p_s, p_t = part(CT, 1), part(CT, 1), part(CT, 1)
        l_b, l_s, l_t = part(VT, 1), part(VT, 1), part(VT, 1)
        taps = part(9, VT)
        th1r, th2r = small[:, 0:NH], small[:, NH:2 * NH]
        delta, th1b = small[:, 2 * NH:2 * NH + RES], small[:, 2 * NH + RES:2 * NH + RES + 1]

        x_pairs = A["x"].rearrange("(t i) (p k) n -> t p i (k n)", i=2, p=P)
        o_pairs = out.rearrange("(t i) (p k) n -> t p i (k n)", i=2, p=P)
        o_tiles = out.rearrange("(t i) (p k) n -> t k p i n", i=2, p=P)

        s_w = [sem(f"s_w{kt}") for kt in range(CT)]
        s_wp, s_par, s_gconst = sem("s_wp"), sem("s_par"), sem("s_gconst")
        s_x, s_res = sem("s_x"), sem("s_res")
        s_store = sem("s_store")
        s_kron1, s_kron2, s_c = sem("s_kron1"), sem("s_kron2"), sem("s_c")
        s_whi, s_wlo, s_wphi, s_wplo = sem("s_whi"), sem("s_wlo"), sem("s_wphi"), sem("s_wplo")
        s_ones, s_zero, s_biasmm = sem("s_ones"), sem("s_zero"), sem("s_biasmm")
        s_ready = sem("s_ready")
        s_v_mm, s_qk_mm, s_proj_mm = sem("s_v_mm"), sem("s_qk_mm"), sem("s_proj_mm")
        s_logit_mm, s_vt_mm = sem("s_logit_mm"), sem("s_vt_mm")
        s_mix_mm, s_av_mm = sem("s_mix_mm"), sem("s_av_mm")
        s_gsum_mm, s_gbc_mm = sem("s_gsum_mm"), sem("s_gbc_mm")
        s_v_sb, s_conv0, s_qk_sb, s_exp = sem("s_v_sb"), sem("s_conv0"), sem("s_qk_sb"), sem("s_exp")
        s_xhi, s_vt_sb, s_mix_sb, s_relu = sem("s_xhi"), sem("s_vt_sb"), sem("s_mix_sb"), sem("s_relu")
        s_conv, s_score, s_rinv = sem("s_conv"), sem("s_score"), sem("s_rinv")
        s_out, s_add, s_olo = sem("s_out"), sem("s_add"), sem("s_olo")
        s_bst, s_mv, s_msq, s_stat = sem("s_bst"), sem("s_mv"), sem("s_msq"), sem("s_stat")
        s_gs, s_gmsq, s_gvar = sem("s_gs"), sem("s_gmsq"), sem("s_gvar")
        s_gval, s_ab, s_xn = sem("s_gval"), sem("s_ab"), sem("s_xn")
        s_qhi_act, s_qhi_pool = sem("s_qhi_act"), sem("s_qhi_pool")
        s_qlo = sem("s_qlo")
        s_khi, s_klo = sem("s_khi"), sem("s_klo")
        s_res_free = sem("s_res_free")
        s_resb, s_rstd, s_xlo, s_mixw = sem("s_resb"), sem("s_rstd"), sem("s_xlo"), sem("s_mixw")

        block = ctx.enter_context(nc.Block())
        N_PAR_DMA = 7

        def keys(img, b):
            return probs[0:HP, img, b, :].rearrange("p (r w) -> p r w", w=PITCH)[:, :, 0:RES]

        def group(b):
            return b // 4

        def mixed(kt, g):
            return ((slice(None), slice(None), kt, slice(g * RES, (g + 1) * RES)),
                    q[:, kt, :].rearrange("p (b i) -> p b i", i=RES))

        POOL_HEADS = 5

        USES = [("vt", 0), ("mix", 0), ("vt", 1), ("mix", 1), ("vt", 2), ("mix", 2), ("vt", 3), ("mix", 3),
                ("mix", 4), ("mix", 5), ("mix", 6)]

        def logit_bank(n):
            return (psL if n % 4 < 2 else psM)[0:HP, n % 2, :]

        def mix_bank(use):
            return (psM if use % 4 < 2 else psL)[0:HALF, use % 2, :]

        def t_has_next(t):
            return not isinstance(t, int) or t < PAIRS - 1

        def wait_alone(eng, semaphore, value):
            eng.wait_ge(semaphore, value)
            eng.nop(nofuse=True)

        def rounds(eng, step):
            step(0, True, False)
            with eng.Fori(1, PAIRS - 1) as t:
                step(t, False, False)
            step(PAIRS - 1, False, True)

        @block.sync
        def _(sp):
            def load_x(t):
                sp.dma_start(xs[:, :, :, :].rearrange("p i k n -> p i (k n)"), x_pairs[t]).then_inc(s_x, 16)

            load_x(0)
            sp.dma_start(g_sum[:, :], A["g_sum"]).then_inc(s_gconst, 16)
            sp.dma_start(g_bc[:, :], A["g_bc"]).then_inc(s_gconst, 16)
            w_rows = A["wqkv"].rearrange("(p k) m -> k p m", p=P)
            for kt in range(CT):
                sp.dma_start(stage_w[:, kt, :], w_rows[kt]).then_inc(s_w[kt], 16)
            for dst, src in ((par[:, :], A["par"]), (th1[:, :, :], A["th1"]), (small[:, :], A["small"]),
                             (abx[:, :], A["abx"]), (ident[:, :], A["ident"]),
                             (mixw[HP:HP + 1, 0, :, :], A["th2b"]), (mixw[HP:HP + 1, 1, :, :], A["th2b"])):
                sp.dma_start(dst, src).then_inc(s_par, 16)
            sp.dma_start(stage_p, A["wp"].rearrange("(k p) m -> p k m", p=P)).then_inc(s_wp, 16)

            def residual(t):
                wait_alone(sp, s_logit_mm, 14 * PAIRS if isinstance(t, int) else 14 * (t + 1))
                sp.dma_start(res.rearrange("p i k n -> p i (k n)"), x_pairs[t - 1]).then_inc(s_res, 16)

            sp.nop(nofuse=True).then_inc(s_res_free, 1)

            def store(t):
                sp.wait_ge(s_out, 3 * t + 1)
                sp.dma_start(o_pairs[t - 1], res.rearrange("p i k n -> p i (k n)")).then_inc(s_store, 16)
                sp.wait_ge(s_store, 16 * t)
                sp.nop(nofuse=True).then_inc(s_res_free, 1)

            def step(t, first, last):
                if not last:
                    sp.wait_ge(s_xhi, t + 1)
                    sp.wait_ge(s_xlo, t + 1)
                    load_x(t + 1)
                if not first:
                    residual(t)
                    store(t)
            rounds(sp, step)
            residual(PAIRS)
            for m in range(CT):
                sp.wait_ge(s_out, 3 * (PAIRS - 1) + m + 2)
                sp.dma_start(o_tiles[PAIRS - 1, m], res[:, :, m, :]).then_inc(s_store, 16)
            sp.wait_ge(s_store, 16 * (PAIRS - 1 + CT))

        @block.tensor
        def _(pe):
            def split3(dst, wlo, whi, rlo, rhi, begin, end):
                for n, (w, r) in enumerate(((wlo, rhi), (whi, rlo), (whi, rhi))):
                    last = nc.tensor.matmul(dst, w, r, start=(begin and n == 0), stop=(end and n == 2))
                return last

            def qkv_tile(m, n):
                for c in range(CT):
                    col = slice(n * P, (n + 1) * P)
                    last = split3(psA[:, m % 2, 0:COLS], w_lo[:, c, col], w_hi[:, c, col],
                                  x_lo[:, :, c, :], x_hi[:, :, c, :], c == 0, c == CT - 1)
                return last

            def group_sums(p):
                pe.wait_ge(s_stat, p + 1)
                nc.tensor.matmul(psP[0:GROUPS, 1, 0:4], g_sum[:, :], mv[:, :, :].rearrange("p i s -> p (i s)"),
                                 start=True, stop=True).then_inc(s_gsum_mm, 1)

            def group_broadcast(p):
                pe.wait_ge(s_gval, p + 1)
                nc.tensor.matmul(psP[:, 1, 8:12], g_bc[:, :], g_val[:, :, :].rearrange("p i s -> p (i s)"),
                                 start=True, stop=True).then_inc(s_gbc_mm, 1)

            def project(t, m):
                if m == 0:
                    pe.wait_ge(s_out, 3 * (t - 1) + 1)
                elif m == 1:
                    pe.wait_ge(s_ab, t + 2 if t_has_next(t) else PAIRS)
                else:
                    pe.wait_ge(s_out, 3 * (t - 1) + 2)
                for c in range(VT):
                    if m == 0 and c % 2 == 0:
                        pe.wait_ge(s_olo, 8 * (t - 1) + 5 + c // 2)
                    col = slice(m * P, (m + 1) * P)
                    last = split3(psP[:, m % 2, 0:COLS], wp_lo[:, c, col], wp_hi[:, c, col],
                                  o_lo[:, c, :], o_hi[:, c, :], c == 0, c == VT - 1)
                last.then_inc(s_proj_mm, 1)

            pe.wait_ge(s_gconst, 32)
            group_sums(0)
            group_broadcast(0)

            def bias_table():
                pe.wait_ge(s_kron1, 1)
                nc.tensor.matmul(psP[0:HP, 0, 0:WINDOW], kron1[:, :, :].rearrange("p g i -> p (g i)"), abx[:, :],
                                 start=True, stop=True).then_inc(s_biasmm, 1)

            def step(t, first, last):
                if first:
                    pe.wait_ge(s_wlo, CT)
                pe.wait_ge(s_xhi, t + 1)
                pe.wait_ge(s_xlo, t + 1)
                for m in range(4):
                    if m >= 2:
                        pe.wait_ge(s_qk_sb, 4 * t + m - 1)
                    elif not first:
                        pe.wait_ge(s_add, 8 * t - 1 + m)
                    qkv_tile(m, m).then_inc(s_qk_mm, 1)
                    if first and m == 0:
                        bias_table()
                for m in range(VT):
                    if m >= 2:
                        pe.wait_ge(s_v_sb, VT * t + m - 1)
                    else:
                        pe.wait_ge(s_qk_sb, 4 * t + 3 + m)
                    qkv_tile(m, 4 + m).then_inc(s_v_mm, 1)
                if not last:
                    group_sums(t + 1)
                pe.wait_ge(s_klo, 2 * (t + 1))
                pe.wait_ge(s_qlo, 16 * (t + 1))
                for n in range(RES):
                    img, b0 = n // 7, 2 * (n % 7)
                    if n >= 4:
                        pe.wait_ge(s_score, 28 * t + 2 * n - 6)
                    elif not first:
                        pe.wait_ge(s_mix_sb, 14 * (t - 1) + 11 + n)
                    for b in (b0, b0 + 1):
                        for kt in range(QT):
                            px = slice(img * PIX, (img + 1) * PIX)
                            mm = split3(logit_bank(n)[:, (b - b0) * PIX:(b - b0 + 1) * PIX],
                                        q_lo[:, img * RES + b, kt, :], q_hi[:, img * RES + b, kt, :],
                                        k_lo[:, kt, px], k_hi[:, kt, px], kt == 0, kt == QT - 1)
                    mm.then_inc(s_logit_mm, 1)
                    if n == 6 and not last:
                        group_broadcast(t + 1)
                if not first:
                    project(t, 0)

                def bank_free(use):
                    if use < 4:
                        pe.wait_ge(s_score, 28 * t + 22 + 2 * use)
                        return
                    i, (what, n) = (use - 4) // 11, USES[(use - 4) % 11]
                    if what == "vt":
                        pe.wait_ge(s_vt_sb, 8 * t + 4 * i + n + 1)
                    else:
                        pe.wait_ge(s_mix_sb, 14 * t + 7 * i + n + 1)

                for use in range(22):
                    img, (what, n) = use // 11, USES[use % 11]
                    bank_free(use)
                    if what == "vt":
                        jc, cg = divmod(n, 2)
                        for c in range(4):
                            at_ = PITCH + 1 + img * PITCH * PITCH + jc * HALF
                            mm = nc.tensor.transpose(mix_bank(use)[:, c * P:(c + 1) * P],
                                                     vpad[:, 4 * cg + c, at_:at_ + HALF], ident[:, :])
                        mm.then_inc(s_vt_mm, 1)
                    else:
                        pe.wait_ge(s_exp, 28 * t + 14 * img + 2 * n + 2)
                        pe.wait_ge(s_mixw, 8 * t + 4 * img + group(2 * n + 1) + 1)
                        bank = mix_bank(use)[:, 0:4 * HP].rearrange("p (j g b i) -> p j g b i", j=2, g=NH, b=2)
                        for jc in range(2):
                            for b in range(2):
                                mm = nc.tensor.matmul(bank[:, jc, :, b, :],
                                                      probs[0:HP + 1, img, 2 * n + b, jc * HALF:(jc + 1) * HALF],
                                                      mixw[0:HP + 1, img, 2 * n + b, :].rearrange("p (g i) -> p g i", g=NH),
                                                      start=True, stop=True)
                        mm.then_inc(s_mix_mm, 1)
                if not first:
                    project(t, 1)
                    project(t, 2)
                else:
                    pe.wait_ge(s_wplo, 1)
                for img in range(2):
                    pe.wait_ge(s_vt_sb, 8 * t + 4 * img + 4)
                    pe.wait_ge(s_mix_sb, 14 * t + 7 * img + 7)
                    for n in range(4):
                        u = 4 * img + n
                        if u < 2:
                            pe.wait_ge(s_v_sb, VT * t + 7 + u)
                        else:
                            pe.wait_ge(s_add, 8 * t + u - 1)
                        for e in range(2):
                            g = 2 * n + e
                            for jc in range(2):
                                mm = nc.tensor.matmul(psA[:, u % 2, e * PIX:(e + 1) * PIX],
                                                      vt[0:HALF, img, jc, g * D:(g + 1) * D], attn[:, img, jc, g, :],
                                                      start=(jc == 0), stop=(jc == 1))
                        mm.then_inc(s_av_mm, 1)
            rounds(pe, step)
            for m in range(CT):
                project(PAIRS, m)

        @block.scalar
        def _(act):
            def x_high(p):
                act.wait_ge(s_xn, 2 * (p + 1))
                nc.scalar.copy(x_hi[:, :, :, :], xs[:, :, :, :]).then_inc(s_xhi, 1)

            def weights_high(kt):
                act.wait_ge(s_w[kt], 16)
                nc.scalar.copy(w_hi[:, kt, :], stage_w[:, kt, :]).then_inc(s_whi, 1)

            weights_high(0)
            weights_high(1)
            weights_high(2)
            x_high(0)

            def conv_centre(t, c):
                act.wait_ge(s_v_sb, VT * t + c + 1)
                if c >= VT // 2:
                    act.wait_ge(s_logit_mm, 14 * t + 7)
                src = vpad[:, c, PITCH + 1:PITCH + 1 + ACC_ROWS * PITCH].rearrange("p (r w) -> p r w", w=PITCH)
                nc.scalar.activation(acc[:, c, :].rearrange("p (r w) -> p r w", w=RES), src[:, :, 0:RES],
                                     ACT.Identity, bias=l_t[:, c:c + 1], scale=taps[:, c, 4:5]).then_inc(s_conv0, 1)

            def relu(t, img, n):
                act.wait_ge(s_add, 8 * t + 4 * img + n + 1)
                nc.scalar.activation(o_hi[:, 2 * n:2 * n + 2, img * PIX:(img + 1) * PIX],
                                     acc[:, 2 * n:2 * n + 2, img * IMG:img * IMG + PIX], ACT.Relu).then_inc(s_relu, 1)

            act.wait_ge(s_ready, 1)

            def mixed_high(t, kt, g):
                act.wait_ge(s_qk_sb, 4 * t + kt + 1)
                dst, src = mixed(kt, g)
                nc.scalar.activation(q_hi[dst], src, ACT.Copy, scale=th1[:, kt, g:g + 1]).then_inc(s_qhi_act, 1)

            def key_high(t, kt):
                act.wait_ge(s_qk_sb, 4 * t + kt + 3)
                nc.scalar.copy(k_hi[:, kt, :], k[:, kt, :]).then_inc(s_khi, 1)

            def step(t, first, last):
                between_qk = {1: [(mixed_high, 0, 5)], 2: [(mixed_high, 0, 6)], 3: [(mixed_high, 0, 7)]}
                between_v = {0: [(mixed_high, 1, 5)], 1: [(conv_centre, 0), (mixed_high, 1, 6)],
                             2: [(conv_centre, 1)], 3: [(mixed_high, 1, 7), (key_high, 0)], 4: [(key_high, 1)],
                             5: [(conv_centre, 2)], 6: [(conv_centre, 3)]}
                for m in range(4):
                    act.wait_ge(s_qk_mm, 4 * t + m + 1)
                    if m == 0 and not first:
                        act.wait_ge(s_qlo, 16 * t)
                    if m == 2 and not first:
                        act.wait_ge(s_logit_mm, 14 * t)
                    dst = q[:, m, :] if m < 2 else k[:, m - 2, :]
                    nc.scalar.activation(dst, psA[:, m % 2, 0:COLS], ACT.Identity, bias=qkv_t[:, m:m + 1],
                                         scale=qkv_s[:, m:m + 1]).then_inc(s_qk_sb, 1)
                    if m == 1:
                        if first:
                            act.wait_ge(s_wlo, CT)
                        else:
                            act.wait_ge(s_av_mm, 8 * t)
                    for what, *args in between_qk.get(m, ()):
                        what(t, *args)
                if not first:
                    act.wait_ge(s_vt_mm, 8 * t)
                    act.wait_ge(s_conv, 64 * t)
                    act.wait_ge(s_olo, 8 * t)
                else:
                    act.wait_ge(s_zero, 1)
                for m in range(VT):
                    act.wait_ge(s_v_mm, VT * t + m + 1)
                    at_ = PITCH + 1
                    dst = vpad[:, m, at_:at_ + 2 * PITCH * PITCH].rearrange("p (i r w) -> p i r w", i=2, w=PITCH)
                    nc.scalar.activation(dst[:, :, 0:RES, 0:RES],
                                         psA[:, m % 2, 0:COLS].rearrange("p (i r w) -> p i r w", i=2, w=RES),
                                         ACT.Identity, bias=qkv_t[:, 4 + m:5 + m],
                                         scale=qkv_s[:, 4 + m:5 + m]).then_inc(s_v_sb, 1)
                    for what, *args in between_v.get(m, ()):
                        what(t, *args)
                if first:
                    act.wait_ge(s_wp, 16)
                    nc.scalar.copy(wp_hi[:, :, :], stage_p).then_inc(s_wphi, 1)
                CENTRES = {15: 4, 17: 5, 19: 6, 21: 7}
                if not first:
                    act.wait_ge(s_rinv, 2 * t)
                for n in range(2 * RES):
                    img, b = divmod(n, RES)
                    act.wait_ge(s_score, 28 * t + n + 1)
                    row = keys(img, b)
                    nc.scalar.activation(row, row, ACT.Exp,
                                         bias=nmax[:, img, b:b + 1], scale=-1.0,
                                         accum_out=rowsum[:, img, b:b + 1]).then_inc(s_exp, 1)
                    if n in CENTRES:
                        conv_centre(t, CENTRES[n])
                for use in range(22):
                    img, (what, n) = use // 11, USES[use % 11]
                    if what == "vt":
                        jc, cg = divmod(n, 2)
                        act.wait_ge(s_vt_mm, 8 * t + 4 * img + n + 1)
                        if use == 0 and not first:
                            act.wait_ge(s_av_mm, 8 * t)
                        nc.scalar.copy(vt[0:HALF, img, jc, cg * BANK:(cg + 1) * BANK],
                                       mix_bank(use)).then_inc(s_vt_sb, 1)
                    else:
                        act.wait_ge(s_mix_mm, 14 * t + 7 * img + n + 1)
                        src = mix_bank(use)[:, 0:4 * HP].rearrange("p (j g m) -> p j g m", j=2, g=NH)
                        nc.scalar.copy(attn[:, img, :, :, 2 * n * RES:(2 * n + 2) * RES], src).then_inc(s_mix_sb, 1)
                if not last:
                    act.wait_ge(s_v_mm, VT * (t + 1))
                    x_high(t + 1)
                if not first:
                    act.wait_ge(s_proj_mm, 3 * t)
                for img in range(2):
                    for n in range(4):
                        relu(t, img, n)
            rounds(act, step)

        @block.vector
        def _(dve):
            nc.vector.memset(mhalf[:, :], -0.5)

            def constants():
                dve.wait_ge(s_par, 16 * N_PAR_DMA)
                for dst, src, signal in ((kron2, th2r, s_kron2), (kron1, th1r, s_kron1)):
                    nc.vector.tensor_tensor(dst[:, :, :], src.unsqueeze(2).broadcast_to([HP, NH, RES]),
                                            delta.unsqueeze(1).broadcast_to([HP, NH, RES]), MUL).then_inc(signal, 1)
                nc.vector.tensor_tensor(qkv_b, qkv_b, qkv_s, MUL)
                nc.vector.tensor_tensor(p_b, p_b, p_s, MUL)
                nc.vector.tensor_tensor(l_b, l_b, l_s, MUL)
                nc.vector.tensor_scalar(th1[:, :, :], th1[:, :, :], SCALE, None, MUL)
                nc.vector.tensor_tensor(taps, taps, l_s.unsqueeze(2).broadcast_to([P, VT, 9]), MUL).then_inc(s_c, 1)
                dve.wait_ge(s_c, 1)
                nc.vector.tensor_tensor(qkv_t, qkv_t, qkv_b, ADD)
                nc.vector.tensor_tensor(p_t, p_t, p_b, ADD)
                nc.vector.tensor_tensor(l_t, l_t, l_b, ADD).then_inc(s_ready, 1)

            def stats(p):
                dve.wait_ge(s_x, 16 * (p + 1))
                for n in range(4):
                    i, half = divmod(n, 2)
                    run = CT * PIX // 2
                    src = xs[:, i, :, :].rearrange("p k n -> p (k n)")
                    nc.vector.bn_stats(bst[:, i, half, :], src[:, half * run:(half + 1) * run]).then_inc(s_bst, 1)
                wait_alone(dve, s_bst, 4 * (p + 1))
                for i in range(2):
                    nc.vector.bn_aggr(mv[:, i, :], bst[:, i, :, :]).then_inc(s_mv, 1)
                dve.wait_ge(s_mv, 2 * (p + 1))
                nc.vector.tensor_tensor(mean_sq[:, :], mv[:, :, 0], mv[:, :, 0], MUL).then_inc(s_msq, 1)
                dve.wait_ge(s_msq, p + 1)
                nc.vector.tensor_tensor(mv[:, :, 1], mv[:, :, 1], mean_sq[:, :], ADD).then_inc(s_stat, 1)

            def group_variance(p, n):
                if n == 0:
                    dve.wait_ge(s_gsum_mm, p + 1)
                    nc.vector.tensor_copy(gs[:, :, :].rearrange("p i s -> p (i s)"), psP[0:GROUPS, 1, 0:4]).then_inc(s_gs, 1)
                elif n == 1:
                    dve.wait_ge(s_gs, p + 1)
                    nc.vector.tensor_tensor(g_msq[:, :], gs[:, :, 0], gs[:, :, 0], MUL).then_inc(s_gmsq, 1)
                else:
                    dve.wait_ge(s_gmsq, p + 1)
                    nc.vector.scalar_tensor_tensor(g_var[:, :], gs[:, :, 1], EPS, g_msq[:, :], ADD, SUB).then_inc(s_gvar, 1)

            def group_values(p):
                dve.wait_ge(s_rstd, p + 1)
                nc.vector.scalar_tensor_tensor(g_val[0:GROUPS, :, 1], gs[:, :, 0], -1.0, g_val[0:GROUPS, :, 0],
                                               MUL, MUL).then_inc(s_gval, 1)

            def channel_values(p):
                dve.wait_ge(s_gbc_mm, p + 1)
                nc.vector.tensor_copy(ab[:, :, :].rearrange("p i s -> p (i s)"), psP[:, 1, 8:12]).then_inc(s_ab, 1)

            def weights_low(kt):
                dve.wait_ge(s_whi, kt + 1)
                nc.vector.tensor_tensor(w_lo[:, kt, :], stage_w[:, kt, :], w_hi[:, kt, :].bitcast(f32),
                                        SUB).then_inc(s_wlo, 1)

            stats(0)
            for n in range(3):
                group_variance(0, n)
            group_values(0)
            weights_low(0)
            channel_values(0)
            for i in range(2):
                dve.wait_ge(s_ab, 1)
                nc.vector.tensor_scalar(xs[:, i, :, :], xs[:, i, :, :], ab[:, i, 0:1], ab[:, i, 1:2], MUL, ADD).then_inc(s_xn, 1)
            weights_low(1)
            dve.wait_ge(s_xhi, 1)
            nc.vector.tensor_tensor(x_lo[:, :, :, :], xs[:, :, :, :],
                                    x_hi[:, :, :, :].bitcast(f32), SUB).then_inc(s_xlo, 1)
            constants()
            dve.wait_ge(s_biasmm, 1)
            nc.vector.tensor_scalar(bias[:, :], psP[0:HP, 0, 0:WINDOW], th1b, None, ADD).then_inc(s_out, 1)

            def conv(t, first, c0, n):
                tap, e = divmod(n, 2)
                c = c0 + e
                if tap == 0:
                    dve.wait_ge(s_conv0, VT * t + c + 1)
                else:
                    dve.wait_ge(s_conv, 64 * t + 8 * c0 + 2 * (tap - 1) + e + 1)
                dy, dx = divmod(TAPS[tap], 3)
                at_ = dy * PITCH + dx
                src = vpad[:, c, at_:at_ + ACC_ROWS * PITCH].rearrange("p (r w) -> p r w", w=PITCH)[:, :, 0:RES]
                a = acc[:, c, :].rearrange("p (r w) -> p r w", w=RES)
                nc.vector.scalar_tensor_tensor(a, src, taps[:, c, TAPS[tap]:TAPS[tap] + 1], a, MUL, ADD).then_inc(s_conv, 1)

            def project_out(t, m):
                dve.wait_ge(s_resb, 3 * (t - 1) + m + 1)
                dve.wait_ge(s_proj_mm, 3 * (t - 1) + m + 1)
                nc.vector.scalar_tensor_tensor(res[:, :, m, :], psP[:, m % 2, 0:COLS].rearrange("p (i n) -> p i n", i=2),
                                               p_s[:, m:m + 1], res[:, :, m, :], MUL, ADD).then_inc(s_out, 1)

            def step(t, first, last):
                todo = iter([(c, n) for c in range(0, VT, 2) for n in range(16)])

                def convs(count):
                    for _ in range(count):
                        nxt = next(todo, None)
                        if nxt:
                            conv(t, first, *nxt)

                if not last:
                    stats(t + 1)
                if not first:
                    dve.wait_ge(s_olo, 8 * t)
                    dve.wait_ge(s_av_mm, 8 * t)
                    dve.wait_ge(s_res_free, t)
                low_half = iter([(kt, g) for kt in range(QT) for g in range(NH)])

                def mixed_low(count):
                    for _ in range(count):
                        kt, g = next(low_half)
                        if g < POOL_HEADS:
                            dve.wait_ge(s_qhi_pool, 10 * t + 5 * kt + g + 1)
                        else:
                            dve.wait_ge(s_qhi_act, 6 * t + 3 * kt + g - POOL_HEADS + 1)
                        dst, src = mixed(kt, g)
                        nc.vector.scalar_tensor_tensor(q_lo[dst], src, th1[:, kt, g:g + 1], q_hi[dst].bitcast(f32),
                                                       MUL, SUB).then_inc(s_qlo, 1)

                mixed_low(14)
                convs(4)
                mixed_low(2)
                convs(8)
                if first:
                    dve.wait_ge(s_out, 1)
                    dve.wait_ge(s_ones, 1)
                else:
                    dve.wait_ge(s_mix_mm, 14 * t)
                for n in range(RES):
                    wait_alone(dve, s_logit_mm, 14 * t + n + 1)
                    for r in (2 * n, 2 * n + 1):
                        img, b = divmod(r, RES)
                        at_ = (RES - 1 - b) * RES
                        nc.vector.tensor_tensor_reduce(
                            out=keys(img, b),
                            in0=logit_bank(n)[:, (r % 2) * PIX:(r % 2 + 1) * PIX].rearrange("p (r w) -> p r w", w=RES),
                            in1=bias[:, at_:at_ + PIX].rearrange("p (r w) -> p r w", w=RES),
                            scale=-1.0, scalar=3.4028234e38, op0=ADD, op1=ALU.min,
                            accum_out=nmax[:, img, b:b + 1]).then_inc(s_score, 1)
                    if n < 3 and not last:
                        group_variance(t + 1, n)
                    elif n == 4 and not last:
                        group_values(t + 1)
                    elif n == 8 and not last:
                        channel_values(t + 1)
                    elif n == 10:
                        dve.wait_ge(s_exp, 28 * t + 14)
                        if not first:
                            dve.wait_ge(s_mixw, 8 * t)
                        nc.vector.reciprocal(rinv[:, 0, :], rowsum[:, 0, :]).then_inc(s_rinv, 1)
                    convs(1)
                convs(6)
                dve.wait_ge(s_exp, 28 * t + 28)
                nc.vector.reciprocal(rinv[:, 1, :], rowsum[:, 1, :]).then_inc(s_rinv, 1)
                convs(12)
                if not first:
                    project_out(t, 0)
                convs(64)
                if not first:
                    project_out(t, 1)
                    project_out(t, 2)
                if first:
                    dve.wait_ge(s_wplo, 1)
                else:
                    dve.wait_ge(s_proj_mm, 3 * t)

                def low(u):
                    img, n = divmod(u, 4)
                    dve.wait_ge(s_relu, 8 * t + u + 1)
                    a = acc[:, 2 * n:2 * n + 2, img * IMG:img * IMG + PIX]
                    sl = (slice(None), slice(2 * n, 2 * n + 2), slice(img * PIX, (img + 1) * PIX))
                    nc.vector.scalar_tensor_tensor(o_lo[sl], a, 0.0, o_hi[sl].bitcast(f32), ALU.max, SUB).then_inc(s_olo, 1)

                for u in range(8):
                    img, n = divmod(u, 4)
                    dve.wait_ge(s_conv, 64 * t + 16 * (n + 1))
                    dve.wait_ge(s_av_mm, 8 * t + u + 1)
                    a = acc[:, 2 * n:2 * n + 2, img * IMG:img * IMG + PIX]
                    nc.vector.tensor_tensor(a, psA[:, n % 2, 0:COLS].rearrange("p (c n) -> p c n", c=2), a,
                                            ADD).then_inc(s_add, 1)
                    if u:
                        low(u - 1)
                low(7)
            rounds(dve, step)
            for m in range(CT):
                project_out(PAIRS, m)

        @block.gpsimd
        def _(pool):
            nc.gpsimd.memset(vpad[:, :, :], 0.0).then_inc(s_zero, 1)
            nc.gpsimd.memset(probs[:, :, :, :], 1.0).then_inc(s_ones, 1)

            def rstd(p):
                pool.wait_ge(s_gvar, p + 1)
                nc.gpsimd.tensor_tensor(g_val[0:GROUPS, :, 0], g_var[:, :], mhalf[:, :], ALU.pow).then_inc(s_rstd, 1)

            def normalise(p):
                wait_alone(pool, s_ab, p + 1)
                for i in range(2):
                    nc.gpsimd.tensor_scalar(xs[:, i, :, :], xs[:, i, :, :], ab[:, i, 0:1], ab[:, i, 1:2],
                                            MUL, ADD).then_inc(s_xn, 1)

            def x_low(p):
                pool.wait_ge(s_xhi, p + 1)
                nc.gpsimd.tensor_tensor(x_lo[:, :, :, :], xs[:, :, :, :],
                                        x_hi[:, :, :, :].bitcast(f32), SUB).then_inc(s_xlo, 1)

            def residual_bias(t):
                wait_alone(pool, s_res, 16 * t)
                for m in range(CT):
                    nc.gpsimd.tensor_scalar(res[:, :, m, :], res[:, :, m, :], p_t[:, m:m + 1], 1.0,
                                            ADD, MUL).then_inc(s_resb, 1)

            def mixing_weights(t, first, img):
                if not first:
                    pool.wait_ge(s_mix_mm, 14 * (t - 1) + 7 * (img + 1))
                pool.wait_ge(s_rinv, 2 * t + img + 1)
                for b0 in range(0, RES, 4):
                    nb = min(4, RES - b0)
                    k2 = kron2[:, :, :].rearrange("p g i -> p (g i)").unsqueeze(1).broadcast_to([HP, nb, HP])
                    nc.gpsimd.tensor_tensor(mixw[0:HP, img, b0:b0 + nb, :], k2,
                                            rinv[:, img, b0:b0 + nb].unsqueeze(2).broadcast_to([HP, nb, HP]),
                                            MUL).then_inc(s_mixw, 1)

            rstd(0)
            pool.wait_ge(s_whi, CT)
            nc.gpsimd.tensor_tensor(w_lo[:, 2, :], stage_w[:, 2, :], w_hi[:, 2, :].bitcast(f32), SUB).then_inc(s_wlo, 1)
            pool.wait_ge(s_ready, 1)
            pool.wait_ge(s_wlo, CT)

            def step(t, first, last):
                if not first:
                    pool.wait_ge(s_av_mm, 8 * t)
                for kt in range(QT):
                    wait_alone(pool, s_qk_sb, 4 * t + kt + 1)
                    for g in range(POOL_HEADS):
                        dst, src = mixed(kt, g)
                        nc.gpsimd.tensor_scalar(q_hi[dst], src, th1[:, kt, g:g + 1], 1.0, MUL, MUL).then_inc(s_qhi_pool, 1)
                for kt in range(QT):
                    wait_alone(pool, s_khi, 2 * t + kt + 1)
                    nc.gpsimd.tensor_tensor(k_lo[:, kt, :], k[:, kt, :], k_hi[:, kt, :].bitcast(f32),
                                            SUB).then_inc(s_klo, 1)
                if not last:
                    rstd(t + 1)
                    normalise(t + 1)
                mixing_weights(t, first, 0)
                mixing_weights(t, first, 1)
                if first:
                    pool.wait_ge(s_wphi, 1)
                    nc.gpsimd.tensor_tensor(wp_lo[:, :, :], stage_p, wp_hi[:, :, :].bitcast(f32), SUB).then_inc(s_wplo, 1)
                else:
                    residual_bias(t)
                if not last:
                    pool.wait_ge(s_v_mm, VT * (t + 1))
                    x_low(t + 1)
            rounds(pool, step)
            residual_bias(PAIRS)


def kernel(**inputs):
    import concourse.bacc as bacc
    from concourse.bass_utils import run_bass_kernel_spmd

    a = {n.replace("L0_conv_", ""): np.asarray(v) for n, v in inputs.items()}

    def tiles(v):
        return v.reshape(-1, P).T

    def threes(v):
        return v.reshape(P, CT)

    def triple(f):
        return np.concatenate([tiles(a[f("q")]), tiles(a[f("k")]), tiles(a[f("v")])], axis=1)

    eye = np.eye(P, dtype=np.float32)
    member = (np.arange(P)[:, None] // (GC // CT) == np.arange(GROUPS)[None, :]).astype(np.float32)
    rows = np.abs(np.arange(2 * RES - 1) - (RES - 1))[None, :, None] * RES
    offs = rows + np.abs(np.arange(RES)[:, None, None] - np.arange(RES)[None, None, :])
    arrays = {
        "x": a["x"].reshape(BATCH, DIM, PIX),
        "wqkv": np.concatenate([a["qw"], a["kw"], a["vw"]], axis=0).T,
        "wp": a["pw"].T.reshape(DH, P, CT).transpose(0, 2, 1).reshape(DH, DIM),
        "par": np.concatenate([triple(lambda n: n + "b"), triple(lambda n: n + "_s"), triple(lambda n: n + "_t"),
                               threes(a["pb"]), threes(a["p_s"]), threes(a["p_t"]),
                               tiles(a["lvb"]), tiles(a["lv_s"]), tiles(a["lv_t"]),
                               a["lvw"].reshape(VT, P, 9).transpose(1, 0, 2).reshape(P, VT * 9)], axis=1),
        "th1": np.repeat(a["th1w"].T.reshape(QT, HR, NH), KD, axis=1).transpose(1, 0, 2),
        "ident": eye,
        "g_sum": member * np.float32(CT / GC),
        "g_bc": member.T,
        "small": np.concatenate([np.repeat(a["th1w"].T, RES, axis=0), np.repeat(a["th2w"].T, RES, axis=0),
                                 np.tile(np.eye(RES, dtype=np.float32), (NH, 1)),
                                 np.repeat(a["th1b"], RES)[:, None]], axis=1),
        "abx": a["ab"][:, offs].reshape(HP, WINDOW),
        "th2b": np.tile(np.repeat(a["th2b"], RES), RES).reshape(1, RES, HP),
    }
    nc = bacc.Bacc("TRN2", target_bir_lowering=False, num_devices=1, dynamic_dma_scratch_size=1024)
    feeds, aps = {}, {}
    for name, v in arrays.items():
        v = np.ascontiguousarray(v)
        feeds[f"in_{name}"] = v
        aps[name] = nc.dram_tensor(f"in_{name}", v.shape, mybir.dt.from_np(v.dtype), kind="ExternalInput").ap()
    out = nc.dram_tensor("out", (BATCH, DIM, PIX), mybir.dt.float32, kind="ExternalOutput").ap()
    build(nc, aps, out)
    r = run_bass_kernel_spmd(nc, [feeds], core_ids=[0])
    return r.results[0]["out"].reshape(BATCH, DIM, RES, RES)
```
